# Optimizing a Trainium2 kernel written in Bass

```python
import numpy as np
import jax
import jax.numpy as jnp

def _softmax(x, axis=-1):
    return jax.nn.softmax(x, axis=axis)

def _gelu(x):
    return jax.nn.gelu(x, approximate=True)

def _silu(x):
    return jax.nn.silu(x)

def _sigmoid(x):
    return jax.nn.sigmoid(x)

def _layernorm(x, axis=-1, eps=1e-05):
    m = jnp.mean(x, axis=axis, keepdims=True)
    v = jnp.var(x, axis=axis, keepdims=True)
    return (x - m) / jnp.sqrt(v + eps)

def _scatter_add(tgt, idx, src, axis=0):
    return tgt.at[idx].add(src)

def _segment_sum(src, seg, n):
    return jax.ops.segment_sum(src, seg, n)
kernel_name = 'mk_adj_resnorm_d2_adj_r2_8b9ff2'

def setup_inputs(seed: int=0):
    np.random.seed(seed)
    _w = jnp.asarray

    def _rec_inputs():
        import jax
        import jax.numpy as jnp
        _gk = jax.random.key(seed)
        x = -0.0001538 + 1 * jax.random.normal(jax.random.fold_in(_gk, 1), (128, 64, 384), jnp.float32)
        _w = (1.0 + jnp.arange(64, dtype=jnp.float32)) ** (-0.5)
        _w = _w / _w.mean()
        _pij = jnp.clip(0.125 * _w[:, None] * _w[None, :], 0.0, 1.0)
        _a = jax.random.uniform(jax.random.fold_in(_gk, 2), (128, 64, 64)) < _pij
        _a = jnp.logical_or(_a, jnp.eye(64, dtype=bool))
        adj = _a
        return (x, adj)
    x, adj = _rec_inputs()

    def _L0_gnn_setup():
        import jax, jax.numpy as jnp
        import numpy as np
        B, S, H = (4, 1024, 384)
        NUM_HEADS = 6
        HEAD_SIZE = H // NUM_HEADS
        NEG = -9000000000000000.0

        def _heads(x):
            b, s, _ = x.shape
            return x.reshape(b, s, NUM_HEADS, HEAD_SIZE).transpose(0, 2, 1, 3)
        key = jax.random.key(seed)
        ks = jax.random.split(key, 10)
        seq_inputs = jax.random.normal(ks[0], (B, S, H), dtype=jnp.float32)
        gm = jax.random.randint(ks[1], (B, S, S), 0, 2) > 0
        graph_mask = gm | jnp.eye(S, dtype=bool)[None]
        sc = 1.0 / np.sqrt(H)
        Wq = jax.random.normal(ks[2], (H, H), dtype=jnp.float32) * sc
        bq = jnp.zeros((H,), dtype=jnp.float32)
        Wk = jax.random.normal(ks[3], (H, H), dtype=jnp.float32) * sc
        bk = jnp.zeros((H,), dtype=jnp.float32)
        Wv = jax.random.normal(ks[4], (H, H), dtype=jnp.float32) * sc
        bv = jnp.zeros((H,), dtype=jnp.float32)
        Wf = jax.random.normal(ks[5], (H, H), dtype=jnp.float32) * sc
        bf = jnp.zeros((H,), dtype=jnp.float32)
        return {'seq_inputs': seq_inputs, 'Wq': Wq, 'bq': bq, 'Wk': Wk, 'bk': bk, 'Wv': Wv, 'bv': bv, 'Wf': Wf, 'bf': bf, 'graph_mask': graph_mask}
    _L0_gnn_all = _L0_gnn_setup()
    _L0_gnn_in = {k: v for k, v in _L0_gnn_all.items() if k in ('Wq', 'bq', 'Wk', 'bk', 'Wv', 'bv', 'Wf', 'bf')}
    del _L0_gnn_all

    def _L1_gnn_setup():
        import jax, jax.numpy as jnp
        import numpy as np
        ATT_HEAD = 12
        IN_DIM = 384
        OUT_DIM = IN_DIM // ATT_HEAD
        LEAKY_ALPHA = 0.2
        B, N = (8, 256)
        key = jax.random.key(seed)
        ks = jax.random.split(key, 8)
        feat_in = jax.random.normal(ks[0], (B, N, IN_DIM), dtype=jnp.float32)
        adj = jax.random.randint(ks[1], (B, N, N), 0, 2) > 0
        lim_W = float(np.sqrt(6.0 / (IN_DIM + OUT_DIM)))
        W = jax.random.uniform(ks[2], (ATT_HEAD, IN_DIM, OUT_DIM), minval=-lim_W, maxval=lim_W, dtype=jnp.float32)
        b = jnp.zeros((OUT_DIM,), dtype=jnp.float32)
        lim_w = float(np.sqrt(6.0 / (OUT_DIM + 1)))
        w_src = jax.random.uniform(ks[3], (ATT_HEAD, OUT_DIM, 1), minval=-lim_w, maxval=lim_w, dtype=jnp.float32)
        w_dst = jax.random.uniform(ks[4], (ATT_HEAD, OUT_DIM, 1), minval=-lim_w, maxval=lim_w, dtype=jnp.float32)
        std_H = float(np.sqrt(2.0 / (IN_DIM + IN_DIM)))
        H_w = jax.random.normal(ks[5], (IN_DIM, IN_DIM), dtype=jnp.float32) * std_H
        H_b = jax.random.normal(ks[6], (IN_DIM,), dtype=jnp.float32) * 0.01
        return {'feat_in': feat_in, 'adj': adj, 'W': W, 'b': b, 'w_src': w_src, 'w_dst': w_dst, 'H_w': H_w, 'H_b': H_b}
    _L1_gnn_all = _L1_gnn_setup()
    _L1_gnn_in = {k: v for k, v in _L1_gnn_all.items() if k in ('W', 'b', 'w_src', 'w_dst', 'H_w', 'H_b')}
    del _L1_gnn_all
    return {'x': x, 'adj': adj, 'L0_gnn_Wq': _L0_gnn_in['Wq'], 'L0_gnn_bq': _L0_gnn_in['bq'], 'L0_gnn_Wk': _L0_gnn_in['Wk'], 'L0_gnn_bk': _L0_gnn_in['bk'], 'L0_gnn_Wv': _L0_gnn_in['Wv'], 'L0_gnn_bv': _L0_gnn_in['bv'], 'L0_gnn_Wf': _L0_gnn_in['Wf'], 'L0_gnn_bf': _L0_gnn_in['bf'], 'L1_gnn_W': _L1_gnn_in['W'], 'L1_gnn_b': _L1_gnn_in['b'], 'L1_gnn_w_src': _L1_gnn_in['w_src'], 'L1_gnn_w_dst': _L1_gnn_in['w_dst'], 'L1_gnn_H_w': _L1_gnn_in['H_w'], 'L1_gnn_H_b': _L1_gnn_in['H_b']}

def reference(x, adj, L0_gnn_Wq, L0_gnn_bq, L0_gnn_Wk, L0_gnn_bk, L0_gnn_Wv, L0_gnn_bv, L0_gnn_Wf, L0_gnn_bf, L1_gnn_W, L1_gnn_b, L1_gnn_w_src, L1_gnn_w_dst, L1_gnn_H_w, L1_gnn_H_b):
    import jax
    import jax.numpy as jnp

    def _L0_gnn_ref(seq_inputs, Wq, bq, Wk, bk, Wv, bv, Wf, bf, graph_mask):
        import jax, jax.numpy as jnp
        import numpy as np
        B, S, H = (4, 1024, 384)
        NUM_HEADS = 6
        HEAD_SIZE = H // NUM_HEADS
        NEG = -9000000000000000.0

        def _heads(x):
            b, s, _ = x.shape
            return x.reshape(b, s, NUM_HEADS, HEAD_SIZE).transpose(0, 2, 1, 3)
        q = _heads(seq_inputs @ Wq + bq)
        k = _heads(seq_inputs @ Wk + bk)
        v = _heads(seq_inputs @ Wv + bv)
        scores = jnp.einsum('bhqd,bhkd->bhqk', q, k) / np.sqrt(HEAD_SIZE)
        bias = jnp.where(graph_mask, 0.0, NEG)[:, None]
        probs = jax.nn.softmax(scores + bias, axis=-1)
        ctx = jnp.einsum('bhqk,bhkd->bhqd', probs, v)
        ctx = ctx.transpose(0, 2, 1, 3).reshape(seq_inputs.shape[0], seq_inputs.shape[1], H)
        return ctx @ Wf + bf

    def _L1_gnn_ref(feat_in, adj, W, b, w_src, w_dst, H_w, H_b):
        import jax, jax.numpy as jnp
        import numpy as np
        ATT_HEAD = 12
        IN_DIM = 384
        OUT_DIM = IN_DIM // ATT_HEAD
        LEAKY_ALPHA = 0.2
        B, N = (8, 256)
        h = jnp.einsum('bnd,ade->bane', feat_in, W)
        th = jnp.tanh(h)
        attn_src = jnp.einsum('bane,aeo->bano', th, w_src)
        attn_dst = jnp.einsum('bane,aeo->bano', th, w_dst)
        attn = attn_src + jnp.swapaxes(attn_dst, 2, 3)
        attn = jnp.where(attn >= 0, attn, LEAKY_ALPHA * attn)
        mask = ~adj[:, None, :, :]
        attn = jnp.where(mask, jnp.float32(-999.0), attn)
        attn = jax.nn.softmax(attn, axis=-1)
        feat_out = jnp.einsum('banm,bame->bane', attn, h) + b
        feat_out = jnp.swapaxes(feat_out, 1, 2).reshape(feat_in.shape[0], feat_in.shape[1], -1)
        feat_out = jax.nn.elu(feat_out)
        gate = jax.nn.sigmoid(feat_in @ H_w.T + H_b)
        return gate * feat_out + (1.0 - gate) * feat_in
    x = _layernorm(x + _L0_gnn_ref(x, L0_gnn_Wq, L0_gnn_bq, L0_gnn_Wk, L0_gnn_bk, L0_gnn_Wv, L0_gnn_bv, L0_gnn_Wf, L0_gnn_bf, adj), axis=-1)
    x = _layernorm(x + _L1_gnn_ref(x, adj, L1_gnn_W, L1_gnn_b, L1_gnn_w_src, L1_gnn_w_dst, L1_gnn_H_w, L1_gnn_H_b), axis=-1)
    return x

_drawn_inputs = setup_inputs


def setup_inputs(seed=0):
    import zlib

    import numpy as np

    out = dict(_drawn_inputs(seed))
    spreads = {'L0_gnn_bq': (0.0, 0.1),
     'L0_gnn_bk': (0.0, 2.0),
     'L0_gnn_bv': (0.0, 0.1),
     'L0_gnn_bf': (0.0, 0.1),
     'L1_gnn_b': (0.0, 0.1)}
    factors = {'L1_gnn_H_b': 33.995}
    for name, (base, spread) in spreads.items():
        noise = np.random.default_rng([zlib.crc32(name.encode()), seed]).standard_normal(out[name].shape)
        drawn = base * np.exp(spread * noise) if base else spread * noise
        out[name] = jnp.asarray(drawn.astype(out[name].dtype))
    for name, factor in factors.items():
        out[name] = (out[name] * factor).astype(out[name].dtype)
    return out
```

```python
import numpy as np
import concourse.bass as bass
from concourse import mybir
from contextlib import ExitStack


def graph_attention_pair(nc, x_tok, x_feat, adj_nodes, wq, bq, wk, bk, wv, bv, wf, bf,
                         w1, b1, w_src, w_dst, hw_t, hb, out):
    F32, F32R, U8 = mybir.dt.float32, mybir.dt.float32r, mybir.dt.uint8
    ALU, ACT, AX = mybir.AluOpType, mybir.ActivationFunctionType, mybir.AxisListType

    P = 128
    TOKENS, D = x_tok.shape
    N = adj_nodes.shape[0]
    KT = D // P
    H0, DH0 = 6, 64
    H1, DH1 = 12, 32
    J0, J1 = H0 // 2, H1 // 2
    G = 2
    B = G * P // N
    C = G * P
    CHUNKS = TOKENS // C
    SCALE = float(DH0) ** -0.5
    NEG = 9000000000000000.0
    MASKED = -999.0
    ALPHA = 0.2
    EPS = 1e-5
    HEADS_PER_TILE = P // DH1
    LAST = 4
    BIAS_LOADS = 16 * (1 + 4 + P // DH1 + 1)
    BIAS0_READY = 7

    ROWS = 2 * HEADS_PER_TILE
    terms_src = nc.dram_tensor("terms_src", (2, 2, KT, 2, C), F32).ap()
    terms_dst = nc.dram_tensor("terms_dst", (2, 2, KT, 2, C), F32).ap()

    ctx = ExitStack()
    with ctx:
        def sb(name, shape, dt=F32):
            return ctx.enter_context(nc.sbuf_tensor(name, shape, dt))

        def pb(name):
            return ctx.enter_context(nc.psum_tensor(name, [P, 512], F32))

        def sem(name):
            return ctx.enter_context(nc.semaphore(name))

        W = {n: (sb(n + "_hi", [P, KT, D], F32R), sb(n + "_lo", [P, KT, D], F32R))
             for n in ("wq", "wk", "wv", "wf", "w1", "hw")}
        ident = sb("ident", [P, P])
        ones = sb("ones", [P, P])
        bq_col, bk_col, bv_col, hb_col = (sb(n, [P, KT]) for n in ("bq_col", "bk_col", "bv_col", "hb_col"))
        hb_half = sb("hb_half", [P, KT])
        b1_col, b1_neg, b1_neg1 = (sb(n, [P, 1]) for n in ("b1_col", "b1_neg", "b1_neg1"))
        bv_rep = sb("bv_rep", [P, KT, P])
        bias0 = sb("bias0", [P, D])
        bf_rep = sb("bf_rep", [P, D])
        w_terms = sb("w_terms", [P, KT, 32])
        masked_val = sb("masked_val", [P, 1])
        power = sb("power", [P, G])
        eps_first, eps_last = sb("eps_first", [P, G]), sb("eps_last", [P, G])

        xt = [sb(f"xt{i}", [P, KT, C]) for i in range(2)]
        xh = [sb(f"xh{i}", [P, KT, C], F32R) for i in range(2)]
        xl = [sb(f"xl{i}", [P, KT, C], F32R) for i in range(2)]
        xtok = [sb(f"xtok{i}", [P, G, D]) for i in range(2)]
        xb = [sb(f"xb{i}", [P, G, D]) for i in range(2)]
        adj = [sb(f"adj{i}", [P, B * N], U8) for i in range(2)]
        bias_m = [sb(f"bias_m{i}", [P, B * N]) for i in range(2)]
        adj1 = [sb(f"adj1_{i}", [P, B * N], U8) for i in range(2)]
        no_edge = sb("no_edge", [P, B * N], U8)
        qT, kT = sb("qT", [P, KT, C]), sb("kT", [P, KT, C])
        v = [sb(f"v{i}", [P, G, D]) for i in range(2)]
        s0 = [sb(f"s0_{i}", [P, G, J0 * P]) for i in range(2)]
        p0T = sb("p0T", [P, G, H0, P])
        st0 = [sb(f"st0_{i}", [P, 3, G, 2 * J0]) for i in range(2)]
        ch = sb("ch", [P, G, KT, P], F32R)
        cl = sb("cl", [P, G, KT, P], F32R)
        y = sb("y", [P, G, D])
        ln = [sb(f"ln{i}", [P, G, 6]) for i in range(2)]
        mv = [sb(f"mv{i}", [P, G, 2]) for i in range(2)]
        ve = [sb(f"ve{i}", [P, G]) for i in range(2)]
        rstd = [sb(f"rstd{i}", [P, G]) for i in range(2)]
        x1 = sb("x1", [P, G, D])
        x1T = [sb(f"x1T{i}", [P, KT, C]) for i in range(2)]
        x1h = sb("x1h", [P, KT, C], F32R)
        x1l = sb("x1l", [P, KT, C], F32R)
        h = [sb(f"h{i}", [P, G, D]) for i in range(2)]
        thT = sb("thT", [P, KT, C])
        gate = [sb(f"gate{i}", [P, KT, C]) for i in range(2)]
        terms = sb("terms", [P, C])
        nbr = [sb(f"nbr{i}", [P, J1, C]) for i in range(2)]
        own_row = [sb(f"own_row{i}", [J1 * B, P]) for i in range(2)]
        own = sb("own", [P, J1 * B])
        a1 = sb("a1", [P, J1, C])
        st1 = sb("st1", [P, 3, J1 * B])
        p1T = sb("p1T", [P, G, H1, P])
        el = sb("el", [P, KT, C])
        u = sb("u", [P, KT, C])
        z = sb("z", [P, KT, C])
        res = [sb(f"res{i}", [P, G, D]) for i in range(2)]
        warm = sb("warm", [P, 1])

        bank = [pb(f"bank{i}") for i in range(8)]

        s_const = sem("s_const")
        s_wload = [sem("s_wload0"), sem("s_wload1")]
        s_bias_load = sem("s_bias_load")
        s_terms_load = sem("s_terms_load")
        s_split = sem("s_split")
        s_prep = sem("s_prep")
        s_prep_mm = sem("s_prep_mm")
        s_x_in = [sem("s_x_in0"), sem("s_x_in1")]
        s_tok_in = [sem("s_tok_in0"), sem("s_tok_in1")]
        s_adj_in = [sem("s_adj_in0"), sem("s_adj_in1")]
        s_adj1_in = [sem("s_adj1_in0"), sem("s_adj1_in1")]
        s_xh, s_xl, s_xb, s_mask, s_no_edge = (sem(n) for n in ("s_xh", "s_xl", "s_xb", "s_mask", "s_no_edge"))
        s_qk, s_qk_sb = sem("s_qk"), sem("s_qk_sb")
        s_v, s_v_sb = sem("s_v"), sem("s_v_sb")
        s_s0, s_s0_sb, s_max0, s_sub0, s_exp0, s_sum0, s_rec0, s_p0 = (
            sem(n) for n in ("s_s0", "s_s0_sb", "s_max0", "s_sub0", "s_exp0", "s_sum0", "s_rec0", "s_p0"))
        s_t0, s_t0_sb, s_pv0, s_ch, s_cl, s_wf = (
            sem(n) for n in ("s_t0", "s_t0_sb", "s_pv0", "s_ch", "s_cl", "s_wf"))
        s_y, s_bn, s_mv, s_ve, s_rstd, s_x1 = (sem(n) for n in ("s_y", "s_bn", "s_mv", "s_ve", "s_rstd", "s_x1"))
        s_x1t, s_x1t_sb, s_x1h, s_x1l = (sem(n) for n in ("s_x1t", "s_x1t_sb", "s_x1h", "s_x1l"))
        s_h, s_h_sb, s_ht, s_th, s_gate, s_gate_sb = (
            sem(n) for n in ("s_h", "s_h_sb", "s_ht", "s_th", "s_gate", "s_gate_sb"))
        s_terms, s_terms_sb, s_scratch, s_nbr, s_own_row, s_own_t, s_own = (
            sem(n) for n in ("s_terms", "s_terms_sb", "s_scratch", "s_nbr", "s_own_row", "s_own_t", "s_own"))
        s_add1, s_lrelu, s_msk1, s_max1, s_sub1, s_exp1, s_sum1, s_rec1, s_p1a = (
            sem(n) for n in ("s_add1", "s_lrelu", "s_msk1", "s_max1", "s_sub1", "s_exp1", "s_sum1", "s_rec1", "s_p1a"))
        s_p1b, s_warm = sem("s_p1b"), sem("s_warm")
        s_t1, s_t1_sb, s_pv1, s_neg, s_el, s_u1, s_u2, s_gated, s_z, s_zt = (
            sem(n) for n in ("s_t1", "s_t1_sb", "s_pv1", "s_neg", "s_el", "s_u1", "s_u2", "s_gated", "s_z", "s_zt"))
        s_bn2, s_mv2, s_ve2, s_rstd2, s_res = (sem(n) for n in ("s_bn2", "s_mv2", "s_ve2", "s_rstd2", "s_res"))
        s_out = [sem("s_out0"), sem("s_out1")]

        stage_w = [t[:, :, :].rearrange("p j t -> p (j t)")[:, 0:KT * D].rearrange("p (k n) -> p k n", n=D) for t in nbr]
        wf_full = a1[:, :, :].rearrange("p j t -> p (j t)")[:, 0:KT * D].rearrange("p (k n) -> p k n", n=D)

        def head3(b):
            return b[:, 0:KT * P].rearrange("p (f t) -> p f t", t=P)

        def blocks(t):
            return t[:, :, :].rearrange("p j (b n) -> p (j b) n", n=N)

        def s0_all(i):
            return s0[i][:, :, :].rearrange("p g (c n) -> p (g c) n", n=N)

        def stat0_out(i, what):
            return st0[i][:, what, :, :].rearrange("p g c -> p (g c)")

        def stat0(i, what):
            return stat0_out(i, what).unsqueeze(2).broadcast_to([P, G * 2 * J0, N])

        HALF1 = J1 * B // 2

        def a1_part(part):
            return blocks(a1)[:, part * HALF1:(part + 1) * HALF1, :]

        def stat1_out(what, part):
            return st1[:, what, part * HALF1:(part + 1) * HALF1]

        def stat1(what, part):
            return stat1_out(what, part).unsqueeze(2).broadcast_to([P, HALF1, N])

        def upto(T, k, per, n):
            return T * per + (n - k * per)

        def wait(eng, s, T, on, k, per, n):
            if on(k):
                eng.wait_ge(s, upto(T, k, per, n))

        def last(T, on, *uses):
            return [(s, upto(T, k, per, n)) for s, k, per, n in uses if on(k)][:1]

        def wait_last(eng, T, on, *uses):
            for s, v in last(T, on, *uses):
                eng.wait_ge(s, v)

        def wait_apart(eng, *waits):
            values = [(s, v if isinstance(v, int) else eng.snap(v)) for s, v in waits]
            eng.wait_ge(s_const, 10)
            for s, v in values:
                eng.wait_ge(s, v)

        def dma_count(sems, T, par, on, k, times=1):
            c = (par + k) % 2
            return [(sems[c], T * (8 * times) + (16 * times - 8 * times * (k + c)))] if on(k) else []

        def wait_dma(eng, sems, T, par, on, k, times=1):
            for s, v in dma_count(sems, T, par, on, k, times):
                eng.wait_ge(s, v)

        def steps(eng, step):
            first = LAST + 2
            end = CHUNKS - 1
            rounds = (end - first) // 2

            def exists(t):
                return lambda k: 0 <= t - k < CHUNKS
            for t in range(first):
                step(t, t % 2, exists(t))
            with eng.Fori(0, rounds) as i:
                for half in range(2):
                    step(i * 2 + (first + half), half, lambda k: True)
            for t in range(first + 2 * rounds, CHUNKS + LAST + 1):
                step(t, t % 2, exists(t))

        block = ctx.enter_context(nc.Block())

        @block.sync
        def _(sp):
            weights = (wq, wk, wv, wf, w1, hw_t)
            for n, w in enumerate(weights):
                if n >= 2:
                    sp.wait_ge(s_split, 2 * (n - 1))
                sp.dma_start(stage_w[n % 2], w.rearrange("(k p) n -> p k n", p=P)).then_inc(s_wload[n % 2], 16)
            sp.dma_start(wf_full, wf.rearrange("(k p) n -> p k n", p=P)).then_inc(s_bias_load, 16)
            for col, b in ((bq_col, bq), (bk_col, bk), (bv_col, bv), (hb_col, hb)):
                sp.dma_start(col[:, :], b.rearrange("(k p) -> p k", p=P), allow_slow_non_contiguous=True).then_inc(s_bias_load, 16)
            for q in range(HEADS_PER_TILE):
                sp.dma_start(b1_col[q * DH1:(q + 1) * DH1, :], b1.rearrange("(e o) -> e o", o=1), allow_slow_non_contiguous=True).then_inc(s_bias_load, 16)
            sp.dma_start(bf_rep[:, :], bf.rearrange("(o n) -> o n", o=1).broadcast_to([P, D])).then_inc(s_bias_load, 16)
            sp.wait_ge(s_const, 10)
            for kind, w in enumerate((w_src, w_dst)):
                wr = w.rearrange("(f a) e -> a e f", a=HEADS_PER_TILE)
                for q in range(HEADS_PER_TILE):
                    c = kind * HEADS_PER_TILE + (q % 2) * 2 + q // 2
                    sp.dma_start(w_terms[q * DH1:(q + 1) * DH1, :, c], wr[q], allow_slow_non_contiguous=True).then_inc(s_terms_load, 16)

            def offset(T, k):
                return (T - k) * C

            def load(T, par, on, k):
                i = (par + k) % 2
                tok = offset(T, k)
                wait(sp, s_xl, T, on, k + 2, 1, 1)
                sp.dma_start(xt[i][:, :, :], x_feat.rearrange("(k p) t -> p k t", p=P)[:, :, bass.ds(tok, C)]).then_inc(s_x_in[i], 16)
                wait(sp, s_mask, T, on, k + 2, 1, 1)
                for half in range(2):
                    sp.dma_start(adj[i][half * N:(half + 1) * N, :], adj_nodes[:, bass.ds(tok, C)]).then_inc(s_adj_in[i], 16)

            def load_tokens(T, par, on, k):
                i, tok = (par + k) % 2, offset(T, k)
                wait(sp, s_xb, T, on, k + 2, 1, 1)
                sp.dma_start(xtok[i][:, :, :], x_tok[bass.ds(tok, C), :].rearrange("(g p) n -> p g n", p=P)
                             ).then_inc(s_tok_in[i], 16)

            def load_adj1(T, par, on, k):
                i, tok = (par + k) % 2, offset(T, k)
                wait(sp, s_no_edge, T, on, k + 2, 1, 1)
                for half in range(2):
                    sp.dma_start(adj1[i][half * N:(half + 1) * N, :],
                                 adj_nodes[:, bass.ds(tok, C)]).then_inc(s_adj1_in[i], 16)

            def exchange(T, par, on, k):
                i = (par + k) % 2
                wait(sp, s_add1, T, on, k + 2, 2, 2)
                wait(sp, s_own_t, T, on, k + 2, 1, 1)
                wait(sp, s_terms_sb, T, on, k, 1, 1)
                for f in range(KT):
                    for kind, scratch in enumerate((terms_src, terms_dst)):
                        r = 32 * f + kind * HEADS_PER_TILE
                        for half in range(2):
                            sp.dma_start(scratch[i, half, f], terms[r + 2 * half:r + 2 * half + 2, :]).then_inc(s_scratch, 16)
                wait(sp, s_scratch, T, on, k, 64 * KT, 64 * KT)
                for half in range(2):
                    rows = terms_dst[i, half].rearrange("f u t -> (f u t)").rearrange("(o n) -> o n", o=1)
                    sp.dma_start(nbr[i][half * N:(half + 1) * N, :, :].rearrange("p j t -> p (j t)"),
                                 rows.broadcast_to([N, J1 * C])).then_inc(s_nbr, 16)
                    sp.dma_start(own_row[i][:, half * N:(half + 1) * N],
                                 terms_src[i, half].rearrange("f u (b n) -> (f u b) n", n=N)).then_inc(s_own_row, 16)

            def step(T, par, on):
                if not isinstance(T, int):
                    for k in (-2, -1, 2, 4):
                        sp.compute_val(offset(T, k))
                        for t in range(KT):
                            sp.compute_val(offset(T, k) * 4)
                    for per, n, k in ((1, 1, 0), (1, 1, 1), (2, 2, 4), (1, 1, 4), (1, 1, 2), (64 * KT, 64 * KT, 2)):
                        sp.compute_val(upto(T, k, per, n))
                if on(-2):
                    load(T, par, on, -2)
                if on(-1):
                    load_tokens(T, par, on, -1)
                if on(2):
                    load_adj1(T, par, on, 2)
                if on(4):
                    i, tok = par, offset(T, 4)
                    wait(sp, s_res, T, on, 4, 2, 2)
                    sp.dma_start(out[bass.ds(tok, C), :].rearrange("(g p) n -> p g n", p=P),
                                 res[i][:, :, :]).then_inc(s_out[i], 16)
                if on(2):
                    exchange(T, par, on, 2)

            for c in range(2):
                load(c - 2, c, lambda k: k == -2, -2)
            load_tokens(-1, 1, lambda k: k == -1, -1)
            steps(sp, step)
            for i in range(2):
                sp.wait_ge(s_out[i], 16 * CHUNKS // 2)

        @block.gpsimd
        def _(pool):
            pool.memset(ident[:, :], 0.0).then_inc(s_const, 1)
            pool.memset(ones[:, :], 1.0).then_inc(s_const, 1)
            pool.memset(masked_val[:, :], MASKED).then_inc(s_const, 1)
            pool.memset(w_terms[:, :, :], 0.0).then_inc(s_const, 1)
            pool.memset(power[:, :], -0.5).then_inc(s_const, 1)
            pool.memset(p0T[:, :, :, :], 0.0).then_inc(s_const, 1)
            pool.memset(p1T[:, :, :, :], 0.0).then_inc(s_const, 1)
            pool.memset(eps_first[:, :], EPS).then_inc(s_const, 1)
            pool.memset(eps_last[:, :], 4 * EPS).then_inc(s_const, 1)
            pool.wait_ge(s_const, 9)
            pool.affine_select(out=ident[:, :], in_=ident[:, :], compare_op=ALU.not_equal, fill=1.0, base=0,
                               pattern=[[-1, P]], channel_multiplier=1).then_inc(s_const, 1)
            pool.wait_ge(s_prep, BIAS0_READY)


            def inputs(T, par, on, k):
                i = (par + k) % 2
                wait(pool, s_xh, T, on, k, 1, 1)
                wait(pool, s_v, T, on, k + 2, 2, 2)
                pool.tensor_tensor(xl[i][:, :, :], xt[i][:, :, :], xh[i][:, :, :].bitcast(F32),
                                   ALU.subtract).then_inc(s_xl, 1)

            def inverse_std(T, on, k, s_moments, s_eps, s_done, n, eps):
                wait(pool, s_moments, T, on, k, 2, 2)
                pool.tensor_tensor(ve[n][:, :], mv[n][:, :, 1], eps, ALU.add).then_inc(s_eps, 1)
                wait(pool, s_eps, T, on, k, 1, 1)
                pool.tensor_tensor(rstd[n][:, :], ve[n][:, :], power[:, :], ALU.pow).then_inc(s_done, 1)

            def step(T, par, on):
                if on(-1):
                    inputs(T, par, on, -1)
                if on(3):
                    for part in range(2):
                        wait(pool, s_max1, T, on, 3, 2, part + 1)
                        pool.tensor_tensor(a1_part(part), a1_part(part), stat1(0, part), ALU.subtract).then_inc(s_sub1, 1)
                if on(0):
                    wait(pool, s_max0, T, on, 0, 1, 1)
                    pool.tensor_tensor(s0_all(par), s0_all(par), stat0(par, 0), ALU.subtract).then_inc(s_sub0, 1)
                if on(3):
                    wait(pool, s_rec1, T, on, 3, 2, 2)
                    pool.tensor_tensor(a1_part(1), a1_part(1), stat1(2, 1), ALU.mult).then_inc(s_p1b, 1)
                if on(0):
                    wait_dma(pool, s_tok_in, T, par, on, 0)
                    wait(pool, s_y, T, on, 2, 2, 2)
                    pool.tensor_tensor(xb[par][:, :, :], xtok[par][:, :, :],
                                       bias0[:, :].unsqueeze(1).broadcast_to([P, G, D]), ALU.add).then_inc(s_xb, 1)
                if on(4):
                    inverse_std(T, on, 4, s_mv2, s_ve2, s_rstd2, 1, eps_last[:, :])
                if on(1):
                    inverse_std(T, on, 1, s_mv, s_ve, s_rstd, 0, eps_first[:, :])

            inputs(-1, 1, lambda k: k == -1, -1)
            steps(pool, step)

        @block.scalar
        def _(act):
            act.wait_ge(s_const, 10)
            act.activation(warm[:, :], ones[:, 0:1], ACT.Exp).then_inc(s_warm, 1)
            act.wait_ge(s_prep, BIAS0_READY)
            act.wait_ge(s_bias_load, BIAS_LOADS)

            def step(T, par, on):
                if on(4):
                    for g in range(G):
                        wait(act, s_pv1, T, on, 4, 2, g + 1)
                        wait(act, s_u1, T, on, 5, 2, 2)
                        act.activation(el[:, :, g * P:(g + 1) * P], head3(bank[2 + g]), ACT.Relu,
                                       bias=b1_neg[:, :], scale=-1.0).then_inc(s_neg, 1)
                    wait(act, s_neg, T, on, 4, 2, 2)
                    act.activation(el[:, :, :], el[:, :, :], ACT.Exp, scale=-1.0).then_inc(s_el, 1)
                if on(0):
                    for m in range(KT):
                        wait(act, s_qk, T, on, 0, 3, m + 1)
                        wait(act, s_s0, T, on, 1, 2, 2)
                        b = bank[m % 2]
                        act.activation(qT[:, m, :], b[:, 0:C], ACT.Identity, bias=bq_col[:, m:m + 1]).then_inc(s_qk_sb, 1)
                        act.activation(kT[:, m, :], b[:, C:2 * C], ACT.Identity, bias=bk_col[:, m:m + 1]).then_inc(s_qk_sb, 1)
                if on(2):
                    for g in range(G):
                        wait(act, s_x1t, T, on, 2, 2, g + 1)
                        wait(act, s_z, T, on, 4, 1, 1)
                        act.activation(x1T[par][:, :, g * P:(g + 1) * P], head3(bank[2 + g]), ACT.Copy).then_inc(s_x1t_sb, 1)
                if on(1):
                    for g in range(G):
                        wait(act, s_t0, T, on, 1, 2, g + 1)
                        wait(act, s_pv0, T, on, 2, 2, g + 1)
                        for b in range(2):
                            r = slice(b * N, (b + 1) * N)
                            act.activation(p0T[r, g, :, r], bank[2 + g][r, 0:J0 * P].rearrange("p (h q) -> p h q", q=N),
                                           ACT.Copy).then_inc(s_t0_sb, 1)
                if on(0):
                    for g in range(G):
                        wait(act, s_v, T, on, 0, 2, g + 1)
                        wait(act, s_pv0, T, on, 2, 2, g + 1)
                        act.activation(v[par][:, g, :], bank[1 - g][:, 0:D], ACT.Copy).then_inc(s_v_sb, 1)
                if on(3):
                    for part in range(2):
                        wait(act, s_sub1, T, on, 3, 2, part + 1)
                        act.activation(a1_part(part), a1_part(part), ACT.Exp).then_inc(s_exp1, 1)
                if on(2):
                    for g in range(G):
                        wait(act, s_h, T, on, 2, 2, g + 1)
                        wait(act, s_pv1, T, on, 4, 2, g + 1)
                        act.activation(h[par][:, g, :], bank[1 - g][:, 0:D], ACT.Copy).then_inc(s_h_sb, 1)
                if on(0):
                    wait(act, s_sub0, T, on, 0, 1, 1)
                    act.activation(s0_all(par), s0_all(par), ACT.Exp).then_inc(s_exp0, 1)
                if on(2):
                    for g in range(G):
                        wait(act, s_ht, T, on, 2, 2, g + 1)
                        wait(act, s_terms, T, on, 3, 1, 1)
                        act.activation(thT[:, :, g * P:(g + 1) * P], head3(bank[2 + g]), ACT.Tanh).then_inc(s_th, 1)
                    for m in range(KT):
                        wait(act, s_gate, T, on, 2, 3, m + 1)
                        wait(act, s_gated, T, on, 4, 1, 1)
                        act.activation(gate[par][:, m, :], bank[1 - m % 2][:, 0:C], ACT.Tanh,
                                       bias=hb_half[:, m:m + 1], scale=0.5).then_inc(s_gate_sb, 1)
                if on(3):
                    for g in range(G):
                        wait(act, s_t1, T, on, 3, 2, g + 1)
                        wait(act, s_pv1, T, on, 4, 2, g + 1)
                        for heads, bk in ((slice(0, 8), bank[4 + 2 * g]), (slice(8, H1), bank[5 + 2 * g])):
                            n = heads.stop - heads.start
                            for b in range(2):
                                r = slice(b * N, (b + 1) * N)
                                act.activation(p1T[r, g, heads, r], bk[r, 0:n * N].rearrange("p (h q) -> p h q", q=N),
                                               ACT.Copy).then_inc(s_t1_sb, 1)
                if on(2):
                    wait(act, s_terms, T, on, 2, 1, 1)
                    wait(act, s_scratch, T, on, 3, 64 * KT, 64 * KT)
                    act.activation(terms[0:96, :], bank[6][0:96, 0:C], ACT.Copy).then_inc(s_terms_sb, 1)

            steps(act, step)

        @block.vector
        def _(dve):
            for n, name in enumerate(W):
                hi, lo = W[name]
                dve.wait_ge(s_wload[n % 2], 16 * (n // 2 + 1))
                dve.tensor_copy(hi[:, :, :], stage_w[n % 2]).then_inc(s_split, 1)
                dve.wait_ge(s_split, 2 * n + 1)
                dve.tensor_tensor(lo[:, :, :], stage_w[n % 2], hi[:, :, :].bitcast(F32), ALU.subtract).then_inc(s_split, 1)
            dve.wait_ge(s_bias_load, BIAS_LOADS)
            dve.wait_ge(s_const, 10)
            for k in range(KT):
                dve.tensor_scalar(bv_rep[:, k, :], ones[:, :], bv_col[:, k:k + 1], None, ALU.mult).then_inc(s_prep, 1)
            dve.tensor_scalar(hb_half[:, :], hb_col[:, :], 0.5, None, ALU.mult).then_inc(s_prep, 1)
            dve.tensor_scalar(b1_neg[:, :], b1_col[:, :], -1.0, None, ALU.mult).then_inc(s_prep, 1)
            dve.tensor_scalar(b1_neg1[:, :], b1_col[:, :], -1.0, -1.0, ALU.mult, ALU.add).then_inc(s_prep, 1)
            dve.wait_ge(s_prep_mm, 1)
            dve.tensor_tensor(bias0[:, :], bank[0][:, 0:D], bf_rep[:, :], ALU.add).then_inc(s_prep, 1)
            dve.wait_ge(s_prep, BIAS0_READY)

            def input_high(T, par, on, k):
                i = (par + k) % 2
                wait_dma(dve, s_x_in, T, par, on, k)
                wait(dve, s_v, T, on, k + 2, 2, 2)
                wait(dve, s_s0_sb, T, on, k + 2, 2, 2)
                dve.tensor_copy(xh[i][:, :, :], xt[i][:, :, :]).then_inc(s_xh, 1)
                wait_dma(dve, s_adj_in, T, par, on, k, 2)
                dve.tensor_scalar(bias_m[i][:, :], adj[i][:, :], 1.0, NEG, ALU.subtract, ALU.mult).then_inc(s_mask, 1)

            def step(T, par, on):
                if on(4):
                    for g in range(G):
                        wait(dve, s_el, T, on, 4, 1, 1)
                        wait(dve, s_u2, T, on, 5, 1, 1)
                        dve.scalar_tensor_tensor(u[:, :, g * P:(g + 1) * P], el[:, :, g * P:(g + 1) * P], b1_neg1[:, :],
                                                 head3(bank[2 + g]), ALU.add, ALU.max).then_inc(s_u1, 1)
                    wait(dve, s_u1, T, on, 4, 2, 2)
                    wait(dve, s_gated, T, on, 5, 1, 1)
                    dve.scalar_tensor_tensor(u[:, :, :], u[:, :, :], b1_col[:, :], x1T[par][:, :, :],
                                             ALU.add, ALU.subtract).then_inc(s_u2, 1)
                    wait(dve, s_u2, T, on, 4, 1, 1)
                    wait(dve, s_gate_sb, T, on, 4, 3, 3)
                    dve.scalar_tensor_tensor(u[:, :, :], gate[par][:, :, :], 1.0, u[:, :, :],
                                             ALU.add, ALU.mult).then_inc(s_gated, 1)
                    wait(dve, s_gated, T, on, 4, 1, 1)
                    wait(dve, s_zt, T, on, 5, 2, 2)
                    dve.scalar_tensor_tensor(z[:, :, :], x1T[par][:, :, :], 4.0, u[:, :, :],
                                             ALU.mult, ALU.add).then_inc(s_z, 1)
                if on(2):
                    wait(dve, s_x1t_sb, T, on, 2, 2, 2)
                    wait(dve, s_gate, T, on, 3, 3, 3)
                    dve.tensor_copy(x1h[:, :, :], x1T[par][:, :, :]).then_inc(s_x1h, 1)
                    wait(dve, s_x1h, T, on, 2, 1, 1)
                    dve.tensor_tensor(x1l[:, :, :], x1T[par][:, :, :], x1h[:, :, :].bitcast(F32), ALU.subtract).then_inc(s_x1l, 1)
                if on(-1):
                    input_high(T, par, on, -1)
                if on(3):
                    wait(dve, s_own_t, T, on, 3, 1, 1)
                    dve.tensor_copy(own[:, :], bank[6][:, 0:J1 * B]).then_inc(s_own, 1)
                    wait(dve, s_own, T, on, 3, 1, 1)
                    wait(dve, s_nbr, T, on, 3, 32, 32)
                    wait(dve, s_t1, T, on, 4, 2, 2)
                    for part in range(2):
                        cols = slice(part * J1 * B // 2, (part + 1) * J1 * B // 2)
                        dve.tensor_tensor(a1_part(part), blocks(nbr[(par + 3) % 2])[:, cols, :],
                                          own[:, cols].unsqueeze(2).broadcast_to([P, J1 * B // 2, N]), ALU.add).then_inc(s_add1, 1)
                    for part in range(2):
                        wait(dve, s_add1, T, on, 3, 2, part + 1)
                        dve.scalar_tensor_tensor(a1_part(part), a1_part(part), ALPHA, a1_part(part),
                                                 ALU.mult, ALU.max).then_inc(s_lrelu, 1)
                    wait_dma(dve, s_adj1_in, T, par, on, 3, 2)
                    wait(dve, s_msk1, T, on, 4, 2, 2)
                    dve.tensor_scalar(no_edge[:, :], adj1[(par + 3) % 2][:, :], 0.0, None, ALU.is_equal).then_inc(s_no_edge, 1)
                if on(1):
                    for g in range(G):
                        wait(dve, s_pv0, T, on, 1, 2, g + 1)
                        wait(dve, s_wf, T, on, 2, 2, g + 1)
                        dve.tensor_copy(ch[:, g, :, :], head3(bank[6 + g])).then_inc(s_ch, 1)
                        wait(dve, s_ch, T, on, 1, 2, g + 1)
                        dve.tensor_tensor(cl[:, g, :, :], head3(bank[6 + g]), ch[:, g, :, :].bitcast(F32), ALU.subtract).then_inc(s_cl, 1)
                if on(3):
                    for part in range(2):
                        j = slice(part * J1 // 2, (part + 1) * J1 // 2)
                        wait_apart(dve, *last(T, on, (s_lrelu, 3, 2, part + 1)), *last(T, on, (s_no_edge, 3, 1, 1)))
                        dve.copy_predicated(a1[:, j, :], no_edge[:, :].unsqueeze(1).broadcast_to([P, J1 // 2, C]),
                                            masked_val[:, :].unsqueeze(2).broadcast_to([P, J1 // 2, C])).then_inc(s_msk1, 1)
                        wait(dve, s_msk1, T, on, 3, 2, part + 1)
                        dve.tensor_reduce(stat1_out(0, part), a1_part(part), AX.X, ALU.max).then_inc(s_max1, 1)
                if on(0):
                    for g in range(G):
                        wait(dve, s_s0, T, on, 0, 2, g + 1)
                        wait(dve, s_mask, T, on, 0, 1, 1)
                        wait(dve, s_t0, T, on, 2, 2, 2)
                        dve.scalar_tensor_tensor(s0[par][:, g, :].rearrange("p (j c) -> p j c", c=P), head3(bank[4 + g]), SCALE,
                                                 bias_m[par][:, g * P:(g + 1) * P].unsqueeze(1).broadcast_to([P, J0, P]),
                                                 ALU.mult, ALU.add).then_inc(s_s0_sb, 1)
                    wait(dve, s_s0_sb, T, on, 0, 2, 2)
                    dve.tensor_reduce(stat0_out(par, 0), s0_all(par), AX.X, ALU.max).then_inc(s_max0, 1)
                if on(3):
                    for part in range(2):
                        wait(dve, s_exp1, T, on, 3, 2, part + 1)
                        dve.tensor_reduce(stat1_out(1, part), a1_part(part), AX.X, ALU.add).then_inc(s_sum1, 1)
                        wait(dve, s_sum1, T, on, 3, 2, part + 1)
                        dve.reciprocal(stat1_out(2, part), stat1_out(1, part)).then_inc(s_rec1, 1)
                    wait(dve, s_rec1, T, on, 3, 2, 1)
                    dve.tensor_tensor(a1_part(0), a1_part(0), stat1(2, 0), ALU.mult).then_inc(s_p1a, 1)
                if on(4):
                    for g in range(G):
                        wait(dve, s_zt, T, on, 4, 2, g + 1)
                        dve.bn_stats(ln[1][:, g, :], bank[2 + g][:, 0:D]).then_inc(s_bn2, 1)
                        wait_apart(dve, *last(T, on, (s_bn2, 4, 2, g + 1)), *last(T, on, (s_res, 5, 2, 2)))
                        dve.bn_aggr(mv[1][:, g, :], ln[1][:, g, :]).then_inc(s_mv2, 1)
                if on(0):
                    wait(dve, s_exp0, T, on, 0, 1, 1)
                    dve.tensor_reduce(stat0_out(par, 1), s0_all(par), AX.X, ALU.add).then_inc(s_sum0, 1)
                    wait(dve, s_sum0, T, on, 0, 1, 1)
                    dve.reciprocal(stat0_out(par, 2), stat0_out(par, 1)).then_inc(s_rec0, 1)
                    wait(dve, s_rec0, T, on, 0, 1, 1)
                    dve.tensor_tensor(s0_all(par), s0_all(par), stat0(par, 2), ALU.mult).then_inc(s_p0, 1)
                if on(4):
                    wait(dve, s_rstd2, T, on, 4, 1, 1)
                    wait_dma(dve, s_out, T, par, on, 6)
                    for g in range(G):
                        dve.tensor_scalar(res[par][:, g, :], bank[2 + g][:, 0:D], mv[1][:, g, 0:1], rstd[1][:, g:g + 1],
                                          ALU.subtract, ALU.mult).then_inc(s_res, 1)
                if on(1):
                    for g in range(G):
                        wait(dve, s_wf, T, on, 1, 2, g + 1)
                        wait(dve, s_xb, T, on, 1, 1, 1)
                        wait(dve, s_x1, T, on, 2, 2, 2)
                        dve.tensor_tensor(y[:, g, :], bank[1 - g][:, 0:D], xb[1 - par][:, g, :], ALU.add).then_inc(s_y, 1)
                    for g in range(G):
                        wait(dve, s_y, T, on, 1, 2, g + 1)
                        dve.bn_stats(ln[0][:, g, :], y[:, g, :]).then_inc(s_bn, 1)
                        wait_apart(dve, *last(T, on, (s_bn, 1, 2, g + 1)))
                        dve.bn_aggr(mv[0][:, g, :], ln[0][:, g, :]).then_inc(s_mv, 1)
                    wait(dve, s_rstd, T, on, 1, 1, 1)
                    wait(dve, s_x1t, T, on, 2, 2, 2)
                    for g in range(G):
                        dve.tensor_scalar(x1[:, g, :], y[:, g, :], mv[0][:, g, 0:1], rstd[0][:, g:g + 1],
                                          ALU.subtract, ALU.mult).then_inc(s_x1, 1)

            input_high(-1, 1, lambda k: k == -1, -1)
            steps(dve, step)

        @block.tensor
        def _(pe):
            pe.wait_ge(s_bias_load, BIAS_LOADS)
            pe.wait_ge(s_prep, KT)
            for k in range(KT):
                mm = pe.matmul(bank[0][:, 0:D], bv_rep[:, k, :], wf_full[:, k, :], start=(k == 0), stop=(k == KT - 1))
            mm.then_inc(s_prep_mm, 1)
            pe.wait_ge(s_split, 2 * len(W))
            pe.wait_ge(s_terms_load, 16 * 2 * HEADS_PER_TILE)
            pe.wait_ge(s_prep, BIAS0_READY)
            pe.wait_ge(s_const, 10)

            def product(out_ap, left, right):
                for k in range(KT):
                    (lh, ll), (rh, rl) = left(k), right(k)
                    pe.matmul(out_ap, lh, rh, start=(k == 0), stop=False)
                    pe.matmul(out_ap, lh, rl, start=False, stop=False)
                    mm = pe.matmul(out_ap, ll, rh, start=False, stop=(k == KT - 1))
                return mm

            def weight(name, cols):
                return lambda k: tuple(w[:, k, cols] for w in W[name])

            def tokens(hi, lo, cols):
                return lambda k: (hi[:, k, cols], lo[:, k, cols])

            def step(T, par, on):
                prev = 1 - par
                if on(0):
                    wait(pe, s_xl, T, on, 0, 1, 1)
                    for m in range(KT):
                        if m == 0:
                            wait_last(pe, T, on, (s_gate_sb, 3, 3, 2), (s_y, 2, 2, 2), (s_v_sb, 1, 2, 2))
                        elif m == 1:
                            wait_last(pe, T, on, (s_gate_sb, 3, 3, 3), (s_y, 2, 2, 1), (s_v_sb, 1, 2, 1))
                        else:
                            wait(pe, s_qk_sb, T, on, 0, 6, 2)
                        fm = slice(m * P, (m + 1) * P)
                        b = bank[m % 2]
                        product(b[:, 0:C], weight("wq", fm), tokens(xh[par], xl[par], slice(0, C)))
                        product(b[:, C:2 * C], weight("wk", fm), tokens(xh[par], xl[par], slice(0, C))).then_inc(s_qk, 1)
                if on(2):
                    for g in range(G):
                        wait(pe, s_x1, T, on, 2, 2, g + 1)
                        wait_last(pe, T, on, (s_u1, 4, 2, g + 1), (s_th, 3, 2, g + 1), (s_t0_sb, 2, 4, 2 * g + 2))
                        for f in range(KT):
                            mm = pe.transpose(bank[2 + g][:, f * P:(f + 1) * P], x1[:, g, f * P:(f + 1) * P], ident[:, :])
                        mm.then_inc(s_x1t, 1)
                if on(3):
                    wait(pe, s_own_row, T, on, 3, 32, 32)
                    wait(pe, s_terms_sb, T, on, 3, 1, 1)
                    pe.matmul(bank[6][:, 0:J1 * B], own_row[prev][:, :], ident[0:J1 * B, 0:J1 * B],
                              start=True, stop=True).then_inc(s_own_t, 1)
                if on(1):
                    wait(pe, s_p0, T, on, 1, 1, 1)
                    for g in range(G):
                        wait(pe, s_x1t_sb, T, on, 2, 2, g + 1)
                        for j in range(J0):
                            mm = pe.transpose(bank[2 + g][:, j * P:(j + 1) * P], s0[prev][:, g, j * P:(j + 1) * P], ident[:, :])
                        mm.then_inc(s_t0, 1)
                if on(0):
                    wait_last(pe, T, on, (s_t1_sb, 4, 8, 4), (s_s0_sb, 1, 2, 2))
                    for g in range(G):
                        wait(pe, s_qk_sb, T, on, 0, 6, 4 + 2 * g)
                        product(bank[1 - g][:, 0:D], tokens(xh[par], xl[par], slice(g * P, (g + 1) * P)),
                                weight("wv", slice(0, D))).then_inc(s_v, 1)
                if on(1):
                    wait(pe, s_v_sb, T, on, 1, 2, 2)
                    for g in range(G):
                        wait(pe, s_t0_sb, T, on, 1, 4, 2 * g + 2)
                        if g == 0:
                            wait_last(pe, T, on, (s_own, 3, 1, 1), (s_cl, 2, 2, 1))
                        else:
                            wait_last(pe, T, on, (s_t1_sb, 4, 8, 8), (s_cl, 2, 2, 2))
                        for head in range(H0):
                            for part in range(2):
                                r, c = (head % 2) * DH0 + part * 32, head * DH0 + part * 32
                                mm = pe.matmul(bank[6 + g][r:r + 32, head // 2 * P:(head // 2 + 1) * P],
                                               v[prev][:, g, c:c + 32], p0T[:, g, head, :], start=True, stop=True)
                        mm.then_inc(s_pv0, 1)
                if on(0):
                    for g in range(G):
                        for j in range(J0):
                            for b in range(2):
                                t = slice(g * P + b * N, g * P + (b + 1) * N)
                                for half in range(2):
                                    r = slice(half * DH0, (half + 1) * DH0)
                                    mm = pe.matmul(bank[4 + g][r, (2 * j + b) * N:(2 * j + b + 1) * N],
                                                   qT[r, j, t], kT[r, j, t], start=True, stop=True)
                        mm.then_inc(s_s0, 1)
                if on(4):
                    wait(pe, s_z, T, on, 4, 1, 1)
                    for g in range(G):
                        wait_last(pe, T, on, (s_t0_sb, 1, 4, 2 * g + 2), (s_x1t_sb, 2, 2, g + 1), (s_u1, 4, 2, g + 1))
                        for f in range(KT):
                            mm = pe.transpose(bank[2 + g][:, f * P:(f + 1) * P], z[:, f, g * P:(g + 1) * P], ident[:, :])
                        mm.then_inc(s_zt, 1)
                if on(2):
                    wait(pe, s_x1l, T, on, 2, 1, 1)
                    for g in range(G):
                        wait_last(pe, T, on, (s_v_sb, 0, 2, g + 1), (s_gate_sb, 3, 3, 3 - g))
                        product(bank[1 - g][:, 0:D], tokens(x1h, x1l, slice(g * P, (g + 1) * P)),
                                weight("w1", slice(0, D))).then_inc(s_h, 1)
                if on(1):
                    for g in range(G):
                        wait(pe, s_cl, T, on, 1, 2, g + 1)
                        wait_last(pe, T, on, (s_h_sb, 2, 2, g + 1), (s_v_sb, 0, 2, g + 1))
                        product(bank[1 - g][:, 0:D], lambda j: (ch[:, g, j, :], cl[:, g, j, :]),
                                weight("wf", slice(0, D))).then_inc(s_wf, 1)
                if on(2):
                    for g in range(G):
                        wait(pe, s_h_sb, T, on, 2, 2, g + 1)
                        wait_last(pe, T, on, (s_res, 4, 2, g + 1), (s_t0_sb, 1, 4, 2 * g + 2))
                        for f in range(KT):
                            mm = pe.transpose(bank[2 + g][:, f * P:(f + 1) * P], h[par][:, g, f * P:(f + 1) * P], ident[:, :])
                        mm.then_inc(s_ht, 1)
                    for m in range(KT):
                        if m < 2:
                            wait_last(pe, T, on, (s_y, 1, 2, m + 1), (s_h_sb, 2, 2, m + 1))
                        else:
                            wait(pe, s_gate_sb, T, on, 2, 3, 1)
                        product(bank[1 - m % 2][:, 0:C], weight("hw", slice(m * P, (m + 1) * P)),
                                tokens(x1h, x1l, slice(0, C))).then_inc(s_gate, 1)
                if on(3):
                    wait(pe, s_p1a, T, on, 3, 1, 1)
                    wait(pe, s_p1b, T, on, 3, 1, 1)
                    for g in range(G):
                        if g == 0:
                            wait_last(pe, T, on, (s_s0_sb, 0, 2, 2), (s_t1_sb, 4, 8, 4))
                        else:
                            wait_last(pe, T, on, (s_cl, 1, 2, 1), (s_own, 3, 1, 1))
                            wait_last(pe, T, on, (s_cl, 1, 2, 2), (s_t1_sb, 4, 8, 8))
                        for j in range(J1):
                            mm = pe.transpose(bank[4 + 2 * g + j // 4][:, j % 4 * P:(j % 4 + 1) * P],
                                              a1[:, j, g * P:(g + 1) * P], ident[:, :])
                        mm.then_inc(s_t1, 1)
                if on(2):
                    wait(pe, s_th, T, on, 2, 2, 2)
                    wait_last(pe, T, on, (s_t1_sb, 3, 8, 8), (s_cl, 1, 2, 1))
                    for f in range(KT):
                        mm = pe.matmul(bank[6][32 * f:32 * f + 32, 0:C], w_terms[:, f, :], thT[:, f, :], start=True, stop=True)
                    mm.then_inc(s_terms, 1)
                if on(3):
                    for g in range(G):
                        wait(pe, s_t1_sb, T, on, 3, 8, 4 * g + 4)
                        wait_last(pe, T, on, (s_th, 2, 2, g + 1), (s_res, 4, 2, g + 1))
                        for head in range(H1):
                            r = head % HEADS_PER_TILE * DH1
                            mm = pe.matmul(bank[2 + g][r:r + DH1, head // HEADS_PER_TILE * P:(head // HEADS_PER_TILE + 1) * P],
                                           h[prev][:, g, head * DH1:(head + 1) * DH1], p1T[:, g, head, :], start=True, stop=True)
                        mm.then_inc(s_pv1, 1)

            steps(pe, step)


INS = ("x_tok", "x_feat", "adj_nodes", "wq", "bq", "wk", "bk", "wv", "bv", "wf", "bf",
       "w1", "b1", "w_src", "w_dst", "hw_t", "hb")


def kernel(x, adj, L0_gnn_Wq, L0_gnn_bq, L0_gnn_Wk, L0_gnn_bk, L0_gnn_Wv, L0_gnn_bv, L0_gnn_Wf, L0_gnn_bf,
           L1_gnn_W, L1_gnn_b, L1_gnn_w_src, L1_gnn_w_dst, L1_gnn_H_w, L1_gnn_H_b):
    import concourse.bacc as bacc
    from concourse.bass_utils import run_bass_kernel_spmd

    graphs, nodes, dim = x.shape
    x_tok = np.ascontiguousarray(np.asarray(x).reshape(graphs * nodes, dim))
    edges = np.ascontiguousarray(np.asarray(adj).transpose(1, 0, 2)).reshape(nodes, graphs * nodes)
    arrays = dict(zip(INS, (
        x_tok, np.ascontiguousarray(x_tok.T), edges,
        L0_gnn_Wq, L0_gnn_bq, L0_gnn_Wk, L0_gnn_bk, L0_gnn_Wv, L0_gnn_bv, L0_gnn_Wf, L0_gnn_bf,
        np.ascontiguousarray(np.asarray(L1_gnn_W).transpose(1, 0, 2)).reshape(dim, dim),
        L1_gnn_b, np.asarray(L1_gnn_w_src)[:, :, 0], np.asarray(L1_gnn_w_dst)[:, :, 0],
        np.ascontiguousarray(np.asarray(L1_gnn_H_w).T), L1_gnn_H_b)))
    arrays = {n: np.ascontiguousarray(a) for n, a in arrays.items()}
    nc = bacc.Bacc("TRN2", target_bir_lowering=False, num_devices=1)
    args = [nc.dram_tensor(n, a.shape, mybir.dt.from_np(a.dtype), kind="ExternalInput").ap() for n, a in arrays.items()]
    out = nc.dram_tensor("out", x_tok.shape, mybir.dt.float32, kind="ExternalOutput").ap()
    graph_attention_pair(nc, *args, out)
    result = run_bass_kernel_spmd(nc, [arrays], core_ids=[0])
    return result.results[0]["out"].reshape(graphs, nodes, dim)
```

```python
import numpy as np
import concourse.bass as bass
from concourse import mybir
from contextlib import ExitStack


def graph_attention_pair(nc, x_tok, x_feat, adj_nodes, wq, bq, wk, bk, wv, bv, wf, bf,
                         w1, b1, w_src, w_dst, hw_t, hb, out):
    F32, F32R, U8 = mybir.dt.float32, mybir.dt.float32r, mybir.dt.uint8
    ALU, ACT, AX = mybir.AluOpType, mybir.ActivationFunctionType, mybir.AxisListType

    P = 128
    TOKENS, D = x_tok.shape
    N = adj_nodes.shape[0]
    KT = D // P
    H0, DH0 = 6, 64
    H1, DH1 = 12, 32
    J0, J1 = H0 // 2, H1 // 2
    G = 2
    B = G * P // N
    C = G * P
    CHUNKS = TOKENS // C
    SCALE = float(DH0) ** -0.5
    NEG = 9000000000000000.0
    MASKED = -999.0
    ALPHA = 0.2
    EPS = 1e-5
    HEADS_PER_TILE = P // DH1
    LAST = 4
    CONSTS = 11
    BIAS_LOADS = 16 * (1 + 4 + P // DH1 + 1)
    BIAS0_READY = 7

    ROWS = 2 * HEADS_PER_TILE
    scratch = nc.dram_tensor("terms_scratch", (2, KT, ROWS, C), F32).ap()

    ctx = ExitStack()
    with ctx:
        def sb(name, shape, dt=F32):
            return ctx.enter_context(nc.sbuf_tensor(name, shape, dt))

        def pb(name):
            return ctx.enter_context(nc.psum_tensor(name, [P, 512], F32))

        def sem(name):
            return ctx.enter_context(nc.semaphore(name))

        W = {n: (sb(n + "_hi", [P, KT, D], F32R), sb(n + "_lo", [P, KT, D], F32R))
             for n in ("wq", "wk", "wv", "wf", "w1", "hw")}
        ident = sb("ident", [P, P])
        ones = sb("ones", [P, P])
        bq_col, bk_col, bv_col, hb_col = (sb(n, [P, KT]) for n in ("bq_col", "bk_col", "bv_col", "hb_col"))
        hb_half = sb("hb_half", [P, KT])
        b1_col, b1_neg, b1_neg1 = (sb(n, [P, 1]) for n in ("b1_col", "b1_neg", "b1_neg1"))
        bv_rep = sb("bv_rep", [P, KT, P])
        bias0 = sb("bias0", [P, D])
        bf_rep = sb("bf_rep", [P, D])
        w_terms = sb("w_terms", [P, KT, 32])
        masked_val = sb("masked_val", [P, 1])
        power = sb("power", [P, G])
        zero, shift = sb("zero", [P, G]), sb("shift", [P, G])
        eps_first, eps_last = sb("eps_first", [P, G]), sb("eps_last", [P, G])

        xt = [sb(f"xt{i}", [P, KT, C]) for i in range(2)]
        xh = [sb(f"xh{i}", [P, KT, C], F32R) for i in range(2)]
        xl = [sb(f"xl{i}", [P, KT, C], F32R) for i in range(2)]
        xtok = [sb(f"xtok{i}", [P, G, D]) for i in range(2)]
        xb = [sb(f"xb{i}", [P, G, D]) for i in range(2)]
        adj = [sb(f"adj{i}", [P, B * N], U8) for i in range(2)]
        bias_m = [sb(f"bias_m{i}", [P, B * N]) for i in range(2)]
        adj1 = [sb(f"adj1_{i}", [P, B * N], U8) for i in range(2)]
        no_edge = sb("no_edge", [P, B * N], U8)
        qT, kT = sb("qT", [P, KT, C]), sb("kT", [P, KT, C])
        v = [sb(f"v{i}", [P, G, D]) for i in range(2)]
        s0 = [sb(f"s0_{i}", [P, G, J0 * P]) for i in range(2)]
        p0T = sb("p0T", [P, G, H0, P])
        st0 = [sb(f"st0_{i}", [P, 3, G, 2 * J0]) for i in range(2)]
        ch = sb("ch", [P, G, KT, P], F32R)
        cl = sb("cl", [P, G, KT, P], F32R)
        y = sb("y", [P, G, D])
        ln = [sb(f"ln{i}", [P, G, 6]) for i in range(2)]
        mv = [sb(f"mv{i}", [P, G, 2]) for i in range(2)]
        ve = [sb(f"ve{i}", [P, G]) for i in range(2)]
        rstd = [sb(f"rstd{i}", [P, G]) for i in range(2)]
        x1 = sb("x1", [P, G, D])
        x1T = [sb(f"x1T{i}", [P, KT, C]) for i in range(2)]
        x1h = sb("x1h", [P, KT, C], F32R)
        x1l = sb("x1l", [P, KT, C], F32R)
        h = [sb(f"h{i}", [P, G, D]) for i in range(2)]
        thT = sb("thT", [P, KT, C])
        gate = [sb(f"gate{i}", [P, KT, C]) for i in range(2)]
        terms = sb("terms", [P, C])
        nbr = [sb(f"nbr{i}", [P, J1, C]) for i in range(2)]
        own_row = [sb(f"own_row{i}", [J1 * B, P]) for i in range(2)]
        own = sb("own", [P, J1 * B])
        a1 = sb("a1", [P, J1, C])
        st1 = sb("st1", [P, 3, J1 * B])
        p1T = sb("p1T", [P, G, H1, P])
        el = sb("el", [P, KT, C])
        u = sb("u", [P, KT, C])
        z = sb("z", [P, KT, C])
        res = [sb(f"res{i}", [P, G, D]) for i in range(2)]
        warm = sb("warm", [P, 1])

        bank = [pb(f"bank{i}") for i in range(8)]

        LATE_FIRST = (1, 0)

        s_const = sem("s_const")
        s_wload = [sem("s_wload0"), sem("s_wload1")]
        s_bias_load = sem("s_bias_load")
        s_terms_load = sem("s_terms_load")
        s_split = sem("s_split")
        s_prep = sem("s_prep")
        s_prep_mm = sem("s_prep_mm")
        s_x_in = [sem("s_x_in0"), sem("s_x_in1")]
        s_tok_in = [sem("s_tok_in0"), sem("s_tok_in1")]
        s_adj_in = [sem("s_adj_in0"), sem("s_adj_in1")]
        s_adj1_in = [sem("s_adj1_in0"), sem("s_adj1_in1")]
        s_xh, s_xl, s_xb, s_mask, s_no_edge = (sem(n) for n in ("s_xh", "s_xl", "s_xb", "s_mask", "s_no_edge"))
        s_qk, s_qk_sb = sem("s_qk"), sem("s_qk_sb")
        s_v, s_v_sb = sem("s_v"), sem("s_v_sb")
        s_s0, s_s0_sb, s_max0, s_sub0, s_exp0, s_sum0, s_rec0, s_p0 = (
            sem(n) for n in ("s_s0", "s_s0_sb", "s_max0", "s_sub0", "s_exp0", "s_sum0", "s_rec0", "s_p0"))
        s_t0, s_t0_sb, s_pv0, s_ch, s_cl, s_wf = (
            sem(n) for n in ("s_t0", "s_t0_sb", "s_pv0", "s_ch", "s_cl", "s_wf"))
        s_y, s_bn, s_mv, s_ve, s_rstd, s_x1 = (sem(n) for n in ("s_y", "s_bn", "s_mv", "s_ve", "s_rstd", "s_x1"))
        s_x1t, s_x1t_sb, s_x1h, s_x1l = (sem(n) for n in ("s_x1t", "s_x1t_sb", "s_x1h", "s_x1l"))
        s_h, s_h_sb, s_ht, s_th, s_gate, s_gate_sb = (
            sem(n) for n in ("s_h", "s_h_sb", "s_ht", "s_th", "s_gate", "s_gate_sb"))
        s_terms, s_terms_sb, s_scratch, s_nbr, s_own_row, s_own_t, s_own = (
            sem(n) for n in ("s_terms", "s_terms_sb", "s_scratch", "s_nbr", "s_own_row", "s_own_t", "s_own"))
        s_add1, s_lrelu, s_msk1, s_max1, s_sub1, s_exp1, s_sum1, s_rec1, s_p1a = (
            sem(n) for n in ("s_add1", "s_lrelu", "s_msk1", "s_max1", "s_sub1", "s_exp1", "s_sum1", "s_rec1", "s_p1a"))
        s_p1b, s_add1b, s_mean2, s_shift2, s_warm = (sem(n) for n in ("s_p1b", "s_add1b", "s_mean2", "s_shift2", "s_warm"))
        s_t1, s_t1_sb, s_pv1, s_neg, s_el, s_u1, s_u2, s_gated, s_z, s_zt = (
            sem(n) for n in ("s_t1", "s_t1_sb", "s_pv1", "s_neg", "s_el", "s_u1", "s_u2", "s_gated", "s_z", "s_zt"))
        s_bn2, s_mv2, s_ve2, s_rstd2, s_res = (sem(n) for n in ("s_bn2", "s_mv2", "s_ve2", "s_rstd2", "s_res"))
        s_out = [sem("s_out0"), sem("s_out1")]

        stage_w = [t[:, :, :].rearrange("p j t -> p (j t)")[:, 0:KT * D].rearrange("p (k n) -> p k n", n=D) for t in nbr]
        wf_full = a1[:, :, :].rearrange("p j t -> p (j t)")[:, 0:KT * D].rearrange("p (k n) -> p k n", n=D)

        def head3(b):
            return b[:, 0:KT * P].rearrange("p (f t) -> p f t", t=P)

        def blocks(t):
            return t[:, :, :].rearrange("p j (b n) -> p (j b) n", n=N)

        def s0_all(i):
            return s0[i][:, :, :].rearrange("p g (c n) -> p (g c) n", n=N)

        def stat0_out(i, what):
            return st0[i][:, what, :, :].rearrange("p g c -> p (g c)")

        def stat0(i, what):
            return stat0_out(i, what).unsqueeze(2).broadcast_to([P, G * 2 * J0, N])

        HALF1 = J1 * B // 2

        def a1_part(part):
            return blocks(a1)[:, part * HALF1:(part + 1) * HALF1, :]

        def stat1_out(what, part):
            return st1[:, what, part * HALF1:(part + 1) * HALF1]

        def stat1(what, part):
            return stat1_out(what, part).unsqueeze(2).broadcast_to([P, HALF1, N])

        def own_part(part):
            return own[:, part * HALF1:(part + 1) * HALF1].unsqueeze(2).broadcast_to([P, HALF1, N])

        def nbr_part(i, part):
            return blocks(nbr[i])[:, part * HALF1:(part + 1) * HALF1, :]

        def upto(T, k, per, n):
            return T * per + (n - k * per)

        def wait(eng, s, T, on, k, per, n):
            if on(k):
                eng.wait_ge(s, upto(T, k, per, n))

        def last(T, on, *uses):
            return [(s, upto(T, k, per, n)) for s, k, per, n in uses if on(k)][:1]

        def wait_last(eng, T, on, *uses):
            for s, v in last(T, on, *uses):
                eng.wait_ge(s, v)

        def wait_apart(eng, *waits):
            values = [(s, v if isinstance(v, int) else eng.compute_val(v)) for s, v in waits]
            eng.wait_ge(s_const, CONSTS)
            for s, v in values:
                eng.wait_ge(s, v)

        def dma_count(sems, T, par, on, k, times=1):
            c = (par + k) % 2
            return [(sems[c], T * (8 * times) + (16 * times - 8 * times * (k + c)))] if on(k) else []

        def wait_dma(eng, sems, T, par, on, k, times=1):
            for s, v in dma_count(sems, T, par, on, k, times):
                eng.wait_ge(s, v)

        def steps(eng, step):
            first = LAST + 2
            end = CHUNKS - 1
            rounds = (end - first) // 2

            def exists(t):
                return lambda k: 0 <= t - k < CHUNKS
            for t in range(first):
                step(t, t % 2, exists(t))
            with eng.Fori(0, rounds) as i:
                for half in range(2):
                    step(i * 2 + (first + half), half, lambda k: True)
            for t in range(first + 2 * rounds, CHUNKS + LAST + 1):
                step(t, t % 2, exists(t))

        block = ctx.enter_context(nc.Block())

        @block.sync
        def _(sp):
            weights = (wq, wk, wv, wf, w1, hw_t)
            for n, w in enumerate(weights):
                if n >= 2:
                    sp.wait_ge(s_split, 2 * (n - 1))
                sp.dma_start(stage_w[n % 2], w.rearrange("(k p) n -> p k n", p=P)).then_inc(s_wload[n % 2], 16)
            sp.dma_start(wf_full, wf.rearrange("(k p) n -> p k n", p=P)).then_inc(s_bias_load, 16)
            for col, b in ((bq_col, bq), (bk_col, bk), (bv_col, bv), (hb_col, hb)):
                sp.dma_start(col[:, :], b.rearrange("(k p) -> p k", p=P), allow_slow_non_contiguous=True).then_inc(s_bias_load, 16)
            for q in range(HEADS_PER_TILE):
                sp.dma_start(b1_col[q * DH1:(q + 1) * DH1, :], b1.rearrange("(e o) -> e o", o=1), allow_slow_non_contiguous=True).then_inc(s_bias_load, 16)
            sp.dma_start(bf_rep[:, :], bf.rearrange("(o n) -> o n", o=1).broadcast_to([P, D])).then_inc(s_bias_load, 16)
            sp.wait_ge(s_const, CONSTS)
            for kind, w in enumerate((w_src, w_dst)):
                wr = w.rearrange("(f a) e -> a e f", a=HEADS_PER_TILE)
                for q in range(HEADS_PER_TILE):
                    c = kind * HEADS_PER_TILE + (q % 2) * 2 + q // 2
                    sp.dma_start(w_terms[q * DH1:(q + 1) * DH1, :, c], wr[q], allow_slow_non_contiguous=True).then_inc(s_terms_load, 16)

            def offset(T, k):
                return (T - k) * C

            def load(T, par, on, k):
                i = (par + k) % 2
                tok = offset(T, k)
                wait(sp, s_xl, T, on, k + 2, 1, 1)
                sp.dma_start(xt[i][:, :, :], x_feat.rearrange("(k p) t -> p k t", p=P)[:, :, bass.ds(tok, C)]).then_inc(s_x_in[i], 16)
                wait(sp, s_mask, T, on, k + 2, 1, 1)
                for half in range(2):
                    sp.dma_start(adj[i][half * N:(half + 1) * N, :], adj_nodes[:, bass.ds(tok, C)]).then_inc(s_adj_in[i], 16)

            def load_tokens(T, par, on, k):
                i, tok = (par + k) % 2, offset(T, k)
                wait(sp, s_xb, T, on, k + 2, 1, 1)
                sp.dma_start(xtok[i][:, :, :], x_tok[bass.ds(tok, C), :].rearrange("(g p) n -> p g n", p=P)
                             ).then_inc(s_tok_in[i], 16)

            def load_adj1(T, par, on, k):
                i, tok = (par + k) % 2, offset(T, k)
                wait(sp, s_no_edge, T, on, k + 2, 1, 1)
                for half in range(2):
                    sp.dma_start(adj1[i][half * N:(half + 1) * N, :],
                                 adj_nodes[:, bass.ds(tok, C)]).then_inc(s_adj1_in[i], 16)

            def exchange(T, par, on, k):
                i = (par + k) % 2
                wait(sp, s_add1, T, on, k + 2, 1, 1)
                wait(sp, s_add1b, T, on, k + 2, 1, 1)
                wait(sp, s_own_t, T, on, k + 2, 1, 1)
                wait(sp, s_terms_sb, T, on, k, 1, 1)
                for f in range(KT):
                    sp.dma_start(scratch[i, f], terms[32 * f:32 * f + ROWS, :]).then_inc(s_scratch, 16)
                wait(sp, s_scratch, T, on, k, 16 * KT, 16 * KT)
                for half in range(2):
                    sp.dma_start(own_row[i][:, half * N:(half + 1) * N],
                                 scratch[i, :, 2 * half:2 * half + 2].rearrange("f u (b n) -> f (u b) n", n=N)).then_inc(s_own_row, 16)
                for half in range(2):
                    r = HEADS_PER_TILE + 2 * half
                    sp.dma_start(nbr[i][half * N:(half + 1) * N, :, :].rearrange("p (f u) t -> p f (u t)", f=KT),
                                 scratch[i, :, r:r + 2].rearrange("f u t -> f (u t)").unsqueeze(0).broadcast_to([N, KT, 2 * C])
                                 ).then_inc(s_nbr, 16)

            def step(T, par, on):
                if not isinstance(T, int):
                    for k in (-2, -1, 2, 4):
                        sp.compute_val(offset(T, k))
                        for t in range(KT):
                            sp.compute_val(offset(T, k) * 4)
                    for per, n, k in ((1, 1, 0), (1, 1, 1), (2, 2, 4), (1, 1, 4), (1, 1, 2), (16 * KT, 16 * KT, 2)):
                        sp.compute_val(upto(T, k, per, n))
                if on(-2):
                    load(T, par, on, -2)
                if on(-1):
                    load_tokens(T, par, on, -1)
                if on(2):
                    load_adj1(T, par, on, 2)
                if on(4):
                    i, tok = par, offset(T, 4)
                    wait(sp, s_res, T, on, 4, 2, 2)
                    sp.dma_start(out[bass.ds(tok, C), :].rearrange("(g p) n -> p g n", p=P),
                                 res[i][:, :, :]).then_inc(s_out[i], 16)
                if on(2):
                    exchange(T, par, on, 2)

            for c in range(2):
                load(c - 2, c, lambda k: k == -2, -2)
            load_tokens(-1, 1, lambda k: k == -1, -1)
            steps(sp, step)
            for i in range(2):
                sp.wait_ge(s_out[i], 16 * CHUNKS // 2)

        @block.gpsimd
        def _(pool):
            pool.memset(ident[:, :], 0.0).then_inc(s_const, 1)
            pool.memset(ones[:, :], 1.0).then_inc(s_const, 1)
            pool.memset(masked_val[:, :], MASKED).then_inc(s_const, 1)
            pool.memset(w_terms[:, :, :], 0.0).then_inc(s_const, 1)
            pool.memset(power[:, :], -0.5).then_inc(s_const, 1)
            pool.memset(p0T[:, :, :, :], 0.0).then_inc(s_const, 1)
            pool.memset(p1T[:, :, :, :], 0.0).then_inc(s_const, 1)
            pool.memset(eps_first[:, :], EPS).then_inc(s_const, 1)
            pool.memset(eps_last[:, :], 4 * EPS).then_inc(s_const, 1)
            pool.memset(zero[:, :], 0.0).then_inc(s_const, 1)
            pool.wait_ge(s_const, CONSTS - 1)
            pool.affine_select(out=ident[:, :], in_=ident[:, :], compare_op=ALU.not_equal, fill=1.0, base=0,
                               pattern=[[-1, P]], channel_multiplier=1).then_inc(s_const, 1)
            pool.wait_ge(s_prep, BIAS0_READY)


            def input_low(T, par, on, k):
                i = (par + k) % 2
                wait(pool, s_xh, T, on, k, 1, 1)
                wait(pool, s_v, T, on, k + 2, 2, 2)
                pool.tensor_tensor(xl[i][:, :, :], xt[i][:, :, :], xh[i][:, :, :].bitcast(F32),
                                   ALU.subtract).then_inc(s_xl, 1)

            def inverse_std(T, on, k, s_moments, s_eps, s_done, n, eps):
                wait(pool, s_moments, T, on, k, 2, 2)
                pool.tensor_tensor(ve[n][:, :], mv[n][:, :, 1], eps, ALU.add).then_inc(s_eps, 1)
                wait(pool, s_eps, T, on, k, 1, 1)
                pool.tensor_tensor(rstd[n][:, :], ve[n][:, :], power[:, :], ALU.pow).then_inc(s_done, 1)

            def step(T, par, on):
                if on(3):
                    wait(pool, s_own, T, on, 3, 1, 1)
                    wait(pool, s_nbr, T, on, 3, 32, 32)
                    wait(pool, s_t1, T, on, 4, 2, 2)
                    pool.tensor_tensor(a1_part(1), nbr_part(1 - par, 1), own_part(1), ALU.add).then_inc(s_add1b, 1)
                    for part in range(2):
                        wait(pool, s_max1, T, on, 3, 2, part + 1)
                        pool.tensor_tensor(a1_part(part), a1_part(part), stat1(0, part), ALU.subtract).then_inc(s_sub1, 1)
                if on(-1):
                    input_low(T, par, on, -1)
                if on(0):
                    wait(pool, s_max0, T, on, 0, 1, 1)
                    pool.tensor_tensor(s0_all(par), s0_all(par), stat0(par, 0), ALU.subtract).then_inc(s_sub0, 1)
                if on(3):
                    wait(pool, s_rec1, T, on, 3, 2, 2)
                    pool.tensor_tensor(a1_part(1), a1_part(1), stat1(2, 1), ALU.mult).then_inc(s_p1b, 1)
                if on(4):
                    inverse_std(T, on, 4, s_mv2, s_ve2, s_rstd2, 1, eps_last[:, :])
                    wait(pool, s_rstd2, T, on, 4, 1, 1)
                    wait(pool, s_res, T, on, 5, 2, 2)
                    pool.tensor_tensor(ve[1][:, :], mv[1][:, :, 0], rstd[1][:, :], ALU.mult).then_inc(s_mean2, 1)
                    wait(pool, s_mean2, T, on, 4, 1, 1)
                    pool.tensor_tensor(shift[:, :], zero[:, :], ve[1][:, :], ALU.subtract).then_inc(s_shift2, 1)
                if on(0):
                    wait(pool, s_rec0, T, on, 0, 1, 1)
                    pool.tensor_tensor(s0_all(par), s0_all(par), stat0(par, 2), ALU.mult).then_inc(s_p0, 1)
                    wait_dma(pool, s_tok_in, T, par, on, 0)
                    wait(pool, s_y, T, on, 2, 2, 2)
                    pool.tensor_tensor(xb[par][:, :, :], xtok[par][:, :, :],
                                       bias0[:, :].unsqueeze(1).broadcast_to([P, G, D]), ALU.add).then_inc(s_xb, 1)
                if on(1):
                    inverse_std(T, on, 1, s_mv, s_ve, s_rstd, 0, eps_first[:, :])

            input_low(-1, 1, lambda k: k == -1, -1)
            steps(pool, step)

        @block.scalar
        def _(act):
            act.wait_ge(s_const, CONSTS)
            act.activation(warm[:, :], ones[:, 0:1], ACT.Exp).then_inc(s_warm, 1)
            act.wait_ge(s_prep, BIAS0_READY)
            act.wait_ge(s_bias_load, BIAS_LOADS)

            def input_high(T, par, on, k):
                i = (par + k) % 2
                wait_dma(act, s_x_in, T, par, on, k)
                wait(act, s_v, T, on, k + 2, 2, 2)
                act.activation(xh[i][:, :, :], xt[i][:, :, :], ACT.Copy).then_inc(s_xh, 1)

            input_high(-1, 1, lambda k: k == -1, -1)

            def step(T, par, on):
                if on(4):
                    for o, g in enumerate(LATE_FIRST):
                        wait(act, s_pv1, T, on, 4, 2, o + 1)
                        wait(act, s_u1, T, on, 5, 2, 2)
                        act.activation(el[:, :, g * P:(g + 1) * P], head3(bank[2 + g]), ACT.Relu,
                                       bias=b1_neg[:, :], scale=-1.0).then_inc(s_neg, 1)
                    wait(act, s_neg, T, on, 4, 2, 2)
                    act.activation(el[:, :, :], el[:, :, :], ACT.Exp, scale=-1.0).then_inc(s_el, 1)
                if on(0):
                    for m in range(KT):
                        wait(act, s_qk, T, on, 0, 3, m + 1)
                        wait(act, s_s0, T, on, 1, 2, 2)
                        b = bank[m % 2]
                        act.activation(qT[:, m, :], b[:, 0:C], ACT.Identity, bias=bq_col[:, m:m + 1]).then_inc(s_qk_sb, 1)
                        act.activation(kT[:, m, :], b[:, C:2 * C], ACT.Identity, bias=bk_col[:, m:m + 1]).then_inc(s_qk_sb, 1)
                if on(2):
                    for g in range(G):
                        wait(act, s_x1t, T, on, 2, 2, g + 1)
                        wait(act, s_z, T, on, 4, 1, 1)
                        act.activation(x1T[par][:, :, g * P:(g + 1) * P], head3(bank[2 + g]), ACT.Copy).then_inc(s_x1t_sb, 1)
                        wait(act, s_gate, T, on, 3, 3, 3)
                        act.activation(x1h[:, :, g * P:(g + 1) * P], head3(bank[2 + g]), ACT.Copy).then_inc(s_x1h, 1)
                if on(1):
                    for g in range(G):
                        wait(act, s_t0, T, on, 1, 2, g + 1)
                        wait(act, s_pv0, T, on, 2, 2, g + 1)
                        for b in range(2):
                            r = slice(b * N, (b + 1) * N)
                            act.activation(p0T[r, g, :, r], bank[2 + g][r, 0:J0 * P].rearrange("p (h q) -> p h q", q=N),
                                           ACT.Copy).then_inc(s_t0_sb, 1)
                if on(0):
                    for g in range(G):
                        wait(act, s_v, T, on, 0, 2, g + 1)
                        wait(act, s_pv0, T, on, 2, 2, g + 1)
                        act.activation(v[par][:, g, :], bank[1 - g][:, 0:D], ACT.Copy).then_inc(s_v_sb, 1)
                if on(3):
                    for part in range(2):
                        wait(act, s_sub1, T, on, 3, 2, part + 1)
                        act.activation(a1_part(part), a1_part(part), ACT.Exp).then_inc(s_exp1, 1)
                        if part == 0 and on(-1):
                            input_high(T, par, on, -1)
                if on(-1) and not on(3):
                    input_high(T, par, on, -1)
                if on(1):
                    for g in range(G):
                        wait(act, s_pv0, T, on, 1, 2, g + 1)
                        wait(act, s_wf, T, on, 2, 2, g + 1)
                        act.activation(ch[:, g, :, :], head3(bank[6 + g]), ACT.Copy).then_inc(s_ch, 1)
                if on(2):
                    for g in range(G):
                        wait(act, s_h, T, on, 2, 2, g + 1)
                        wait(act, s_pv1, T, on, 4, 2, g + 1)
                        act.activation(h[par][:, g, :], bank[1 - g][:, 0:D], ACT.Copy).then_inc(s_h_sb, 1)
                if on(0):
                    wait(act, s_sub0, T, on, 0, 1, 1)
                    act.activation(s0_all(par), s0_all(par), ACT.Exp).then_inc(s_exp0, 1)
                if on(2):
                    for g in range(G):
                        wait(act, s_ht, T, on, 2, 2, g + 1)
                        wait(act, s_terms, T, on, 3, 1, 1)
                        act.activation(thT[:, :, g * P:(g + 1) * P], head3(bank[2 + g]), ACT.Tanh).then_inc(s_th, 1)
                if on(4):
                    wait(act, s_shift2, T, on, 4, 1, 1)
                    wait_dma(act, s_out, T, par, on, 6)
                    for g in range(G):
                        act.activation(res[par][:, g, :], bank[6 + g][:, 0:D], ACT.Identity,
                                       bias=shift[:, g:g + 1], scale=rstd[1][:, g:g + 1]).then_inc(s_res, 1)
                for m in range(KT):
                    if on(2):
                        wait(act, s_gate, T, on, 2, 3, m + 1)
                        wait(act, s_gated, T, on, 4, 1, 1)
                        act.activation(gate[par][:, m, :], bank[1 - m % 2][:, 0:C], ACT.Tanh,
                                       bias=hb_half[:, m:m + 1], scale=0.5).then_inc(s_gate_sb, 1)
                    if on(2) and m == 0:
                        wait(act, s_terms, T, on, 2, 1, 1)
                        wait(act, s_scratch, T, on, 3, 16 * KT, 16 * KT)
                        act.activation(terms[0:96, :], bank[5][0:96, 0:C], ACT.Copy).then_inc(s_terms_sb, 1)
                    if on(3) and m < G:
                        g = LATE_FIRST[m]
                        wait(act, s_t1, T, on, 3, 2, m + 1)
                        wait(act, s_pv1, T, on, 4, 2, m + 1)
                        for heads, bk in ((slice(0, 8), bank[4 + 2 * g]), (slice(8, H1), bank[5 + 2 * g])):
                            n = heads.stop - heads.start
                            for b in range(2):
                                r = slice(b * N, (b + 1) * N)
                                act.activation(p1T[r, g, heads, r], bk[r, 0:n * N].rearrange("p (h q) -> p h q", q=N),
                                               ACT.Copy).then_inc(s_t1_sb, 1)

            steps(act, step)

        @block.vector
        def _(dve):
            for n, name in enumerate(W):
                hi, lo = W[name]
                dve.wait_ge(s_wload[n % 2], 16 * (n // 2 + 1))
                dve.tensor_copy(hi[:, :, :], stage_w[n % 2]).then_inc(s_split, 1)
                dve.wait_ge(s_split, 2 * n + 1)
                dve.tensor_tensor(lo[:, :, :], stage_w[n % 2], hi[:, :, :].bitcast(F32), ALU.subtract).then_inc(s_split, 1)
            dve.wait_ge(s_bias_load, BIAS_LOADS)
            dve.wait_ge(s_const, CONSTS)
            for k in range(KT):
                dve.tensor_scalar(bv_rep[:, k, :], ones[:, :], bv_col[:, k:k + 1], None, ALU.mult).then_inc(s_prep, 1)
            dve.tensor_scalar(hb_half[:, :], hb_col[:, :], 0.5, None, ALU.mult).then_inc(s_prep, 1)
            dve.tensor_scalar(b1_neg[:, :], b1_col[:, :], -1.0, None, ALU.mult).then_inc(s_prep, 1)
            dve.tensor_scalar(b1_neg1[:, :], b1_col[:, :], -1.0, -1.0, ALU.mult, ALU.add).then_inc(s_prep, 1)
            dve.wait_ge(s_prep_mm, 1)
            dve.tensor_tensor(bias0[:, :], bank[0][:, 0:D], bf_rep[:, :], ALU.add).then_inc(s_prep, 1)
            dve.wait_ge(s_prep, BIAS0_READY)

            def mask0(T, par, on, k):
                i = (par + k) % 2
                wait_dma(dve, s_adj_in, T, par, on, k, 2)
                wait(dve, s_s0_sb, T, on, k + 2, 2, 2)
                dve.tensor_scalar(bias_m[i][:, :], adj[i][:, :], 1.0, NEG, ALU.subtract, ALU.mult).then_inc(s_mask, 1)

            def step(T, par, on):
                if on(4):
                    for g in LATE_FIRST:
                        wait(dve, s_el, T, on, 4, 1, 1)
                        wait(dve, s_gated, T, on, 5, 1, 1)
                        wait(dve, s_z, T, on, 5, 1, 1)
                        dve.scalar_tensor_tensor(u[:, :, g * P:(g + 1) * P], el[:, :, g * P:(g + 1) * P], b1_neg1[:, :],
                                                 head3(bank[2 + g]), ALU.add, ALU.max).then_inc(s_u1, 1)
                    wait(dve, s_u1, T, on, 4, 2, 2)
                    dve.scalar_tensor_tensor(u[:, :, :], u[:, :, :], b1_col[:, :], x1T[par][:, :, :],
                                             ALU.add, ALU.subtract).then_inc(s_u2, 1)
                if on(3):
                    wait_dma(dve, s_adj1_in, T, par, on, 3, 2)
                    wait(dve, s_msk1, T, on, 4, 2, 2)
                    dve.tensor_scalar(no_edge[:, :], adj1[1 - par][:, :], 0.0, None, ALU.is_equal).then_inc(s_no_edge, 1)
                    wait(dve, s_own_t, T, on, 3, 1, 1)
                    wait(dve, s_add1b, T, on, 4, 1, 1)
                    dve.tensor_copy(own[:, :], bank[6][:, 0:J1 * B]).then_inc(s_own, 1)
                if on(4):
                    wait(dve, s_u2, T, on, 4, 1, 1)
                    wait(dve, s_gate_sb, T, on, 4, 3, 3)
                    dve.scalar_tensor_tensor(u[:, :, :], gate[par][:, :, :], 1.0, u[:, :, :],
                                             ALU.add, ALU.mult).then_inc(s_gated, 1)
                if on(3):
                    wait(dve, s_own, T, on, 3, 1, 1)
                    wait(dve, s_nbr, T, on, 3, 32, 32)
                    wait(dve, s_t1, T, on, 4, 2, 2)
                    dve.tensor_tensor(a1_part(0), nbr_part(1 - par, 0), own_part(0), ALU.add).then_inc(s_add1, 1)
                if on(4):
                    wait(dve, s_gated, T, on, 4, 1, 1)
                    wait(dve, s_zt, T, on, 5, 2, 2)
                    dve.scalar_tensor_tensor(z[:, :, :], x1T[par][:, :, :], 4.0, u[:, :, :],
                                             ALU.mult, ALU.add).then_inc(s_z, 1)
                if on(3):
                    for part in range(2):
                        wait(dve, (s_add1, s_add1b)[part], T, on, 3, 1, 1)
                        dve.scalar_tensor_tensor(a1_part(part), a1_part(part), ALPHA, a1_part(part),
                                                 ALU.mult, ALU.max).then_inc(s_lrelu, 1)
                        j = slice(part * J1 // 2, (part + 1) * J1 // 2)
                        wait_apart(dve, *last(T, on, (s_lrelu, 3, 2, part + 1)), *last(T, on, (s_no_edge, 3, 1, 1)))
                        dve.copy_predicated(a1[:, j, :], no_edge[:, :].unsqueeze(1).broadcast_to([P, J1 // 2, C]),
                                            masked_val[:, :].unsqueeze(2).broadcast_to([P, J1 // 2, C])).then_inc(s_msk1, 1)
                        wait(dve, s_msk1, T, on, 3, 2, part + 1)
                        dve.tensor_reduce(stat1_out(0, part), a1_part(part), AX.X, ALU.max).then_inc(s_max1, 1)
                if on(2):
                    wait(dve, s_x1h, T, on, 2, 2, 2)
                    wait(dve, s_gate, T, on, 3, 3, 3)
                    dve.tensor_tensor(x1l[:, :, :], x1T[par][:, :, :], x1h[:, :, :].bitcast(F32), ALU.subtract).then_inc(s_x1l, 1)
                if on(0):
                    for g in range(G):
                        wait(dve, s_s0, T, on, 0, 2, g + 1)
                        wait(dve, s_mask, T, on, 0, 1, 1)
                        wait(dve, s_t0, T, on, 2, 2, 2)
                        dve.scalar_tensor_tensor(s0[par][:, g, :].rearrange("p (j c) -> p j c", c=P), head3(bank[4 + g]), SCALE,
                                                 bias_m[par][:, g * P:(g + 1) * P].unsqueeze(1).broadcast_to([P, J0, P]),
                                                 ALU.mult, ALU.add).then_inc(s_s0_sb, 1)
                if on(3):
                    wait(dve, s_exp1, T, on, 3, 2, 1)
                    dve.tensor_reduce(stat1_out(1, 0), a1_part(0), AX.X, ALU.add).then_inc(s_sum1, 1)
                if on(1):
                    for g in range(G):
                        wait(dve, s_ch, T, on, 1, 2, g + 1)
                        wait(dve, s_wf, T, on, 2, 2, g + 1)
                        dve.tensor_tensor(cl[:, g, :, :], head3(bank[6 + g]), ch[:, g, :, :].bitcast(F32), ALU.subtract).then_inc(s_cl, 1)
                if on(0):
                    wait(dve, s_s0_sb, T, on, 0, 2, 2)
                    dve.tensor_reduce(stat0_out(par, 0), s0_all(par), AX.X, ALU.max).then_inc(s_max0, 1)
                if on(3):
                    wait(dve, s_exp1, T, on, 3, 2, 2)
                    dve.tensor_reduce(stat1_out(1, 1), a1_part(1), AX.X, ALU.add).then_inc(s_sum1, 1)
                    for part in range(2):
                        wait(dve, s_sum1, T, on, 3, 2, part + 1)
                        dve.reciprocal(stat1_out(2, part), stat1_out(1, part)).then_inc(s_rec1, 1)
                    wait(dve, s_rec1, T, on, 3, 2, 1)
                    dve.tensor_tensor(a1_part(0), a1_part(0), stat1(2, 0), ALU.mult).then_inc(s_p1a, 1)
                if on(4):
                    for g in range(G):
                        wait(dve, s_zt, T, on, 4, 2, g + 1)
                        dve.bn_stats(ln[1][:, g, :], bank[6 + g][:, 0:D]).then_inc(s_bn2, 1)
                    for g in range(G):
                        wait_apart(dve, *last(T, on, (s_bn2, 4, 2, g + 1)), *last(T, on, (s_res, 5, 2, 2)))
                        dve.bn_aggr(mv[1][:, g, :], ln[1][:, g, :]).then_inc(s_mv2, 1)
                if on(1):
                    for g in range(G):
                        wait(dve, s_wf, T, on, 1, 2, g + 1)
                        wait(dve, s_xb, T, on, 1, 1, 1)
                        wait(dve, s_x1, T, on, 2, 2, 2)
                        dve.tensor_tensor(y[:, g, :], bank[1 - g][:, 0:D], xb[1 - par][:, g, :], ALU.add).then_inc(s_y, 1)
                if on(0):
                    wait(dve, s_exp0, T, on, 0, 1, 1)
                    dve.tensor_reduce(stat0_out(par, 1), s0_all(par), AX.X, ALU.add).then_inc(s_sum0, 1)
                    wait(dve, s_sum0, T, on, 0, 1, 1)
                    dve.reciprocal(stat0_out(par, 2), stat0_out(par, 1)).then_inc(s_rec0, 1)
                if on(1):
                    for g in range(G):
                        wait(dve, s_y, T, on, 1, 2, g + 1)
                        dve.bn_stats(ln[0][:, g, :], y[:, g, :]).then_inc(s_bn, 1)
                    for g in range(G):
                        wait_apart(dve, *last(T, on, (s_bn, 1, 2, g + 1)))
                        dve.bn_aggr(mv[0][:, g, :], ln[0][:, g, :]).then_inc(s_mv, 1)
                if on(-1):
                    mask0(T, par, on, -1)
                if on(1):
                    wait(dve, s_rstd, T, on, 1, 1, 1)
                    wait(dve, s_x1t, T, on, 2, 2, 2)
                    for g in range(G):
                        dve.tensor_scalar(x1[:, g, :], y[:, g, :], mv[0][:, g, 0:1], rstd[0][:, g:g + 1],
                                          ALU.subtract, ALU.mult).then_inc(s_x1, 1)

            mask0(-1, 1, lambda k: k == -1, -1)
            steps(dve, step)

        @block.tensor
        def _(pe):
            pe.wait_ge(s_bias_load, BIAS_LOADS)
            pe.wait_ge(s_prep, KT)
            for k in range(KT):
                mm = pe.matmul(bank[0][:, 0:D], bv_rep[:, k, :], wf_full[:, k, :], start=(k == 0), stop=(k == KT - 1))
            mm.then_inc(s_prep_mm, 1)
            pe.wait_ge(s_split, 2 * len(W))
            pe.wait_ge(s_terms_load, 16 * 2 * HEADS_PER_TILE)
            pe.wait_ge(s_prep, BIAS0_READY)
            pe.wait_ge(s_const, CONSTS)

            def product(out_ap, left, right):
                for k in range(KT):
                    (lh, ll), (rh, rl) = left(k), right(k)
                    pe.matmul(out_ap, lh, rh, start=(k == 0), stop=False)
                    pe.matmul(out_ap, lh, rl, start=False, stop=False)
                    mm = pe.matmul(out_ap, ll, rh, start=False, stop=(k == KT - 1))
                return mm

            def weight(name, cols):
                return lambda k: tuple(w[:, k, cols] for w in W[name])

            def tokens(hi, lo, cols):
                return lambda k: (hi[:, k, cols], lo[:, k, cols])

            def step(T, par, on):
                prev = 1 - par
                for m in range(KT):
                    if on(0):
                        wait(pe, s_xl, T, on, 0, 1, 1)
                        if m == 0:
                            wait_last(pe, T, on, (s_gate_sb, 3, 3, 2), (s_y, 2, 2, 2), (s_v_sb, 1, 2, 2))
                        elif m == 1:
                            wait_last(pe, T, on, (s_gate_sb, 3, 3, 3), (s_y, 2, 2, 1), (s_v_sb, 1, 2, 1))
                        else:
                            wait(pe, s_qk_sb, T, on, 0, 6, 2)
                        fm = slice(m * P, (m + 1) * P)
                        b = bank[m % 2]
                        product(b[:, 0:C], weight("wq", fm), tokens(xh[par], xl[par], slice(0, C)))
                        product(b[:, C:2 * C], weight("wk", fm), tokens(xh[par], xl[par], slice(0, C))).then_inc(s_qk, 1)
                    if on(3) and m == 1:
                        wait(pe, s_own_row, T, on, 3, 32, 32)
                        wait(pe, s_t1_sb, T, on, 4, 8, 4)
                        pe.matmul(bank[6][:, 0:J1 * B], own_row[prev][:, :], ident[0:J1 * B, 0:J1 * B],
                                  start=True, stop=True).then_inc(s_own_t, 1)
                if on(2):
                    for g in range(G):
                        wait(pe, s_x1, T, on, 2, 2, g + 1)
                        wait_last(pe, T, on, (s_u1, 4, 2, 2), (s_th, 3, 2, g + 1), (s_t0_sb, 2, 4, 2 * g + 2))
                        for f in range(KT):
                            mm = pe.transpose(bank[2 + g][:, f * P:(f + 1) * P], x1[:, g, f * P:(f + 1) * P], ident[:, :])
                        mm.then_inc(s_x1t, 1)
                for g in range(G):
                    if on(0):
                        if g == 0:
                            wait_last(pe, T, on, (s_t1_sb, 4, 8, 8), (s_s0_sb, 1, 2, 2))
                        wait(pe, s_qk_sb, T, on, 0, 6, 4 + 2 * g)
                        product(bank[1 - g][:, 0:D], tokens(xh[par], xl[par], slice(g * P, (g + 1) * P)),
                                weight("wv", slice(0, D))).then_inc(s_v, 1)
                    if on(1) and g == 0:
                        wait(pe, s_p0, T, on, 1, 1, 1)
                        for g0 in range(G):
                            wait(pe, s_x1h, T, on, 2, 2, g0 + 1)
                            for j in range(J0):
                                mm = pe.transpose(bank[2 + g0][:, j * P:(j + 1) * P], s0[prev][:, g0, j * P:(j + 1) * P], ident[:, :])
                            mm.then_inc(s_t0, 1)
                if on(0):
                    for g in range(G):
                        for j in range(J0):
                            for b in range(2):
                                t = slice(g * P + b * N, g * P + (b + 1) * N)
                                for half in range(2):
                                    r = slice(half * DH0, (half + 1) * DH0)
                                    mm = pe.matmul(bank[4 + g][r, (2 * j + b) * N:(2 * j + b + 1) * N],
                                                   qT[r, j, t], kT[r, j, t], start=True, stop=True)
                        mm.then_inc(s_s0, 1)
                if on(1):
                    wait(pe, s_v_sb, T, on, 1, 2, 2)
                    for g in range(G):
                        wait(pe, s_t0_sb, T, on, 1, 4, 2 * g + 2)
                        if g == 0:
                            wait_last(pe, T, on, (s_own, 3, 1, 1), (s_cl, 2, 2, 1))
                        else:
                            wait_last(pe, T, on, (s_t1_sb, 4, 8, 4), (s_cl, 2, 2, 2))
                        for head in range(H0):
                            for part in range(2):
                                r, c = (head % 2) * DH0 + part * 32, head * DH0 + part * 32
                                mm = pe.matmul(bank[6 + g][r:r + 32, head // 2 * P:(head // 2 + 1) * P],
                                               v[prev][:, g, c:c + 32], p0T[:, g, head, :], start=True, stop=True)
                        mm.then_inc(s_pv0, 1)
                if on(2):
                    wait(pe, s_x1l, T, on, 2, 1, 1)
                    for g in range(G):
                        wait_last(pe, T, on, (s_v_sb, 0, 2, g + 1), (s_gate_sb, 3, 3, 3 - g))
                        product(bank[1 - g][:, 0:D], tokens(x1h, x1l, slice(g * P, (g + 1) * P)),
                                weight("w1", slice(0, D))).then_inc(s_h, 1)
                if on(4):
                    wait(pe, s_z, T, on, 4, 1, 1)
                    for g in range(G):
                        wait_last(pe, T, on, (s_cl, 1, 2, g + 1), (s_own, 3, 1, 1), (s_t1_sb, 4, 8, 8))
                        for f in range(KT):
                            mm = pe.transpose(bank[6 + g][:, f * P:(f + 1) * P], z[:, f, g * P:(g + 1) * P], ident[:, :])
                        mm.then_inc(s_zt, 1)
                if on(1):
                    for g in range(G):
                        wait(pe, s_cl, T, on, 1, 2, g + 1)
                        wait_last(pe, T, on, (s_h_sb, 2, 2, g + 1), (s_v_sb, 0, 2, g + 1))
                        product(bank[1 - g][:, 0:D], lambda j: (ch[:, g, j, :], cl[:, g, j, :]),
                                weight("wf", slice(0, D))).then_inc(s_wf, 1)
                if on(2):
                    for g in range(G):
                        wait(pe, s_h_sb, T, on, 2, 2, g + 1)
                        wait_last(pe, T, on, (s_t0_sb, 1, 4, 2 * g + 2), (s_x1h, 2, 2, g + 1))
                        for f in range(KT):
                            mm = pe.transpose(bank[2 + g][:, f * P:(f + 1) * P], h[par][:, g, f * P:(f + 1) * P], ident[:, :])
                        mm.then_inc(s_ht, 1)
                for m in range(KT):
                    if on(2):
                        if m < 2:
                            wait_last(pe, T, on, (s_y, 1, 2, m + 1), (s_h_sb, 2, 2, m + 1))
                        else:
                            wait(pe, s_gate_sb, T, on, 2, 3, 1)
                        product(bank[1 - m % 2][:, 0:C], weight("hw", slice(m * P, (m + 1) * P)),
                                tokens(x1h, x1l, slice(0, C))).then_inc(s_gate, 1)
                    if on(2) and m == 0:
                        wait(pe, s_th, T, on, 2, 2, 2)
                        wait_last(pe, T, on, (s_s0_sb, 0, 2, 2), (s_s0_sb, 1, 2, 2), (s_t1_sb, 4, 8, 8))
                        for f in range(KT):
                            mm = pe.matmul(bank[5][32 * f:32 * f + 32, 0:C], w_terms[:, f, :], thT[:, f, :], start=True, stop=True)
                        mm.then_inc(s_terms, 1)
                    if on(3) and m < G:
                        g = LATE_FIRST[m]
                        wait(pe, s_p1a, T, on, 3, 1, 1)
                        wait(pe, s_p1b, T, on, 3, 1, 1)
                        if g == 0:
                            wait_last(pe, T, on, (s_s0_sb, 0, 2, 2), (s_t1_sb, 4, 8, 8))
                            wait_last(pe, T, on, (s_terms_sb, 2, 1, 1), (s_terms_sb, 3, 1, 1))
                        else:
                            wait_last(pe, T, on, (s_res, 4, 2, 2), (s_cl, 1, 2, 2), (s_own, 3, 1, 1))
                        for j in range(J1):
                            mm = pe.transpose(bank[4 + 2 * g + j // 4][:, j % 4 * P:(j % 4 + 1) * P],
                                              a1[:, j, g * P:(g + 1) * P], ident[:, :])
                        mm.then_inc(s_t1, 1)
                if on(3):
                    for o, g in enumerate(LATE_FIRST):
                        wait(pe, s_t1_sb, T, on, 3, 8, 4 * o + 4)
                        wait_last(pe, T, on, (s_th, 2, 2, g + 1), (s_u1, 4, 2, 2))
                        for head in range(H1):
                            r = head % HEADS_PER_TILE * DH1
                            mm = pe.matmul(bank[2 + g][r:r + DH1, head // HEADS_PER_TILE * P:(head // HEADS_PER_TILE + 1) * P],
                                           h[prev][:, g, head * DH1:(head + 1) * DH1], p1T[:, g, head, :], start=True, stop=True)
                        mm.then_inc(s_pv1, 1)

            steps(pe, step)


INS = ("x_tok", "x_feat", "adj_nodes", "wq", "bq", "wk", "bk", "wv", "bv", "wf", "bf",
       "w1", "b1", "w_src", "w_dst", "hw_t", "hb")


def kernel(x, adj, L0_gnn_Wq, L0_gnn_bq, L0_gnn_Wk, L0_gnn_bk, L0_gnn_Wv, L0_gnn_bv, L0_gnn_Wf, L0_gnn_bf,
           L1_gnn_W, L1_gnn_b, L1_gnn_w_src, L1_gnn_w_dst, L1_gnn_H_w, L1_gnn_H_b):
    import concourse.bacc as bacc
    from concourse.bass_utils import run_bass_kernel_spmd

    graphs, nodes, dim = x.shape
    x_tok = np.ascontiguousarray(np.asarray(x).reshape(graphs * nodes, dim))
    edges = np.ascontiguousarray(np.asarray(adj).transpose(1, 0, 2)).reshape(nodes, graphs * nodes)
    arrays = dict(zip(INS, (
        x_tok, np.ascontiguousarray(x_tok.T), edges,
        L0_gnn_Wq, L0_gnn_bq, L0_gnn_Wk, L0_gnn_bk, L0_gnn_Wv, L0_gnn_bv, L0_gnn_Wf, L0_gnn_bf,
        np.ascontiguousarray(np.asarray(L1_gnn_W).transpose(1, 0, 2)).reshape(dim, dim),
        L1_gnn_b, np.asarray(L1_gnn_w_src)[:, :, 0], np.asarray(L1_gnn_w_dst)[:, :, 0],
        np.ascontiguousarray(np.asarray(L1_gnn_H_w).T), L1_gnn_H_b)))
    arrays = {n: np.ascontiguousarray(a) for n, a in arrays.items()}
    nc = bacc.Bacc("TRN2", target_bir_lowering=False, num_devices=1)
    args = [nc.dram_tensor(n, a.shape, mybir.dt.from_np(a.dtype), kind="ExternalInput").ap() for n, a in arrays.items()]
    out = nc.dram_tensor("out", x_tok.shape, mybir.dt.float32, kind="ExternalOutput").ap()
    graph_attention_pair(nc, *args, out)
    result = run_bass_kernel_spmd(nc, [arrays], core_ids=[0])
    return result.results[0]["out"].reshape(graphs, nodes, dim)
```

```python
import numpy as np
import concourse.bass as bass
from concourse import mybir
from contextlib import ExitStack


def graph_attention_pair(nc, x_tok, x_feat, adj_nodes, wq, bq, wk, bk, wv, bv, wf, bf,
                         w1, b1, w_src, w_dst, hw_t, hb, out):
    F32, F32R, U8 = mybir.dt.float32, mybir.dt.float32r, mybir.dt.uint8
    ALU, ACT, AX = mybir.AluOpType, mybir.ActivationFunctionType, mybir.AxisListType

    P = 128
    TOKENS, D = x_tok.shape
    N = adj_nodes.shape[0]
    KT = D // P
    H0, DH0 = 6, 64
    H1, DH1 = 12, 32
    J0, J1 = H0 // 2, H1 // 2
    G = 2
    B = G * P // N
    C = G * P
    CHUNKS = TOKENS // C
    SCALE = float(DH0) ** -0.5
    NEG = 9000000000000000.0
    MASKED = -999.0
    ALPHA = 0.2
    EPS = 1e-5
    HEADS_PER_TILE = P // DH1
    LAST = 4
    CONSTS = 11
    BIAS_LOADS = 16 * (4 + P // DH1 + 1)
    BIAS0_READY = 7

    ROWS = 2 * HEADS_PER_TILE
    scratch = nc.dram_tensor("terms_scratch", (2, KT, ROWS, C), F32).ap()

    ctx = ExitStack()
    with ctx:
        def sb(name, shape, dt=F32):
            return ctx.enter_context(nc.sbuf_tensor(name, shape, dt))

        def pb(name):
            return ctx.enter_context(nc.psum_tensor(name, [P, 512], F32))

        def sem(name):
            return ctx.enter_context(nc.semaphore(name))

        W = {n: (sb(n + "_hi", [P, KT, D], F32R), sb(n + "_lo", [P, KT, D], F32R))
             for n in ("wq", "wk", "wv", "wf", "w1", "hw")}
        ident = sb("ident", [P, P])
        ones = sb("ones", [P, P])
        bq_col, bk_col, bv_col, hb_col = (sb(n, [P, KT]) for n in ("bq_col", "bk_col", "bv_col", "hb_col"))
        hb_half = sb("hb_half", [P, KT])
        b1_col, b1_neg, b1_neg1 = (sb(n, [P, 1]) for n in ("b1_col", "b1_neg", "b1_neg1"))
        bv_rep = sb("bv_rep", [P, KT, P])
        bias0 = sb("bias0", [P, D])
        bf_rep = sb("bf_rep", [P, D])
        w_terms = sb("w_terms", [P, KT, 32])
        masked_val = sb("masked_val", [P, 1])
        power = sb("power", [P, G])
        zero, shift = sb("zero", [P, G]), sb("shift", [P, G])
        eps_first, eps_last = sb("eps_first", [P, G]), sb("eps_last", [P, G])

        xt = [sb(f"xt{i}", [P, KT, C]) for i in range(2)]
        xh = [sb(f"xh{i}", [P, KT, C], F32R) for i in range(2)]
        xl = [sb(f"xl{i}", [P, KT, C], F32R) for i in range(2)]
        xtok = [sb(f"xtok{i}", [P, G, D]) for i in range(2)]
        xb = [sb(f"xb{i}", [P, G, D]) for i in range(2)]
        adj = [sb(f"adj{i}", [P, B * N], U8) for i in range(2)]
        bias_m = [sb(f"bias_m{i}", [P, B * N]) for i in range(2)]
        adj1 = [sb(f"adj1_{i}", [P, B * N], U8) for i in range(2)]
        no_edge = sb("no_edge", [P, B * N], U8)
        qT, kT = sb("qT", [P, KT, C]), sb("kT", [P, KT, C])
        v = [sb(f"v{i}", [P, G, D]) for i in range(2)]
        s0 = [sb(f"s0_{i}", [P, G, J0 * P]) for i in range(2)]
        p0T = sb("p0T", [P, G, H0, P])
        st0 = [sb(f"st0_{i}", [P, 3, G, 2 * J0]) for i in range(2)]
        ch = sb("ch", [P, G, KT, P], F32R)
        cl = sb("cl", [P, G, KT, P], F32R)
        y = sb("y", [P, G, D])
        ln = [sb(f"ln{i}", [P, G, 6]) for i in range(2)]
        mv = [sb(f"mv{i}", [P, G, 2]) for i in range(2)]
        ve = [sb(f"ve{i}", [P, G]) for i in range(2)]
        rstd = [sb(f"rstd{i}", [P, G]) for i in range(2)]
        x1 = sb("x1", [P, G, D])
        x1T = [sb(f"x1T{i}", [P, KT, C]) for i in range(2)]
        x1h = sb("x1h", [P, KT, C], F32R)
        x1l = sb("x1l", [P, KT, C], F32R)
        h = [sb(f"h{i}", [P, G, D]) for i in range(2)]
        thT = sb("thT", [P, KT, C])
        gate = [sb(f"gate{i}", [P, KT, C]) for i in range(2)]
        terms = sb("terms", [P, C])
        nbr = [sb(f"nbr{i}", [P, J1, C]) for i in range(2)]
        own_row = [sb(f"own_row{i}", [J1 * B, P]) for i in range(2)]
        own = sb("own", [P, J1 * B])
        a1 = sb("a1", [P, J1, C])
        st1 = sb("st1", [P, 3, J1 * B])
        p1T = sb("p1T", [P, G, H1, P])
        el = sb("el", [P, KT, C])
        u = sb("u", [P, KT, C])
        z = sb("z", [P, KT, C])
        res = [sb(f"res{i}", [P, G, D]) for i in range(2)]
        warm = sb("warm", [P, 1])

        bank = [pb(f"bank{i}") for i in range(8)]

        s_const = sem("s_const")
        s_wload = [sem(f"s_wload_{n}") for n in W]
        s_bias_load = sem("s_bias_load")
        s_terms_load = sem("s_terms_load")
        s_high, s_split = sem("s_high"), sem("s_split")
        s_prep = sem("s_prep")
        s_prep_mm = sem("s_prep_mm")
        s_x_in = [sem("s_x_in0"), sem("s_x_in1")]
        s_tok_in = [sem("s_tok_in0"), sem("s_tok_in1")]
        s_adj_in = [sem("s_adj_in0"), sem("s_adj_in1")]
        s_adj1_in = [sem("s_adj1_in0"), sem("s_adj1_in1")]
        s_xh, s_xl, s_xb, s_mask, s_no_edge = (sem(n) for n in ("s_xh", "s_xl", "s_xb", "s_mask", "s_no_edge"))
        s_qk, s_qk_sb = sem("s_qk"), sem("s_qk_sb")
        s_v, s_v_sb = sem("s_v"), sem("s_v_sb")
        s_s0, s_s0_sb, s_max0, s_sub0, s_exp0, s_sum0, s_rec0, s_p0 = (
            sem(n) for n in ("s_s0", "s_s0_sb", "s_max0", "s_sub0", "s_exp0", "s_sum0", "s_rec0", "s_p0"))
        s_t0, s_t0_sb, s_pv0, s_ch, s_cl, s_wf = (
            sem(n) for n in ("s_t0", "s_t0_sb", "s_pv0", "s_ch", "s_cl", "s_wf"))
        s_y, s_bn, s_mv, s_ve, s_rstd, s_x1 = (sem(n) for n in ("s_y", "s_bn", "s_mv", "s_ve", "s_rstd", "s_x1"))
        s_x1t, s_x1t_sb, s_x1h, s_x1l = (sem(n) for n in ("s_x1t", "s_x1t_sb", "s_x1h", "s_x1l"))
        s_h, s_h_sb, s_ht, s_th, s_gate, s_gate_sb = (
            sem(n) for n in ("s_h", "s_h_sb", "s_ht", "s_th", "s_gate", "s_gate_sb"))
        s_terms, s_terms_sb, s_scratch, s_nbr, s_own_row, s_own_t, s_own = (
            sem(n) for n in ("s_terms", "s_terms_sb", "s_scratch", "s_nbr", "s_own_row", "s_own_t", "s_own"))
        s_add1, s_lrelu, s_msk1, s_max1, s_sub1, s_exp1, s_sum1, s_rec1, s_p1a = (
            sem(n) for n in ("s_add1", "s_lrelu", "s_msk1", "s_max1", "s_sub1", "s_exp1", "s_sum1", "s_rec1", "s_p1a"))
        s_p1b, s_add1b, s_mean2, s_shift2, s_warm = (sem(n) for n in ("s_p1b", "s_add1b", "s_mean2", "s_shift2", "s_warm"))
        s_t1, s_t1_sb, s_t1b_sb, s_pv1, s_neg, s_el, s_u1, s_u2, s_gated, s_z, s_zt = (
            sem(n) for n in ("s_t1", "s_t1_sb", "s_t1b_sb", "s_pv1", "s_neg", "s_el", "s_u1", "s_u2", "s_gated", "s_z", "s_zt"))
        s_bn2, s_mv2, s_ve2, s_rstd2, s_res = (sem(n) for n in ("s_bn2", "s_mv2", "s_ve2", "s_rstd2", "s_res"))
        s_out = [sem("s_out0"), sem("s_out1")]

        stage_0, stage_1, wf_full = (t[:, :, :].rearrange("p j t -> p (j t)")[:, 0:KT * D].rearrange("p (k n) -> p k n", n=D)
                                     for t in (*nbr, a1))
        stages = {"wq": stage_0, "wk": stage_1, "wv": stage_0, "wf": wf_full, "w1": stage_1, "hw": stage_0}
        ORDER = list(stages)

        def head3(b):
            return b[:, 0:KT * P].rearrange("p (f t) -> p f t", t=P)

        def blocks(t):
            return t[:, :, :].rearrange("p j (b n) -> p (j b) n", n=N)

        def s0_all(i):
            return s0[i][:, :, :].rearrange("p g (c n) -> p (g c) n", n=N)

        def stat0_out(i, what):
            return st0[i][:, what, :, :].rearrange("p g c -> p (g c)")

        def stat0(i, what):
            return stat0_out(i, what).unsqueeze(2).broadcast_to([P, G * 2 * J0, N])

        HALF1 = J1 * B // 2

        def a1_part(part):
            return blocks(a1)[:, part * HALF1:(part + 1) * HALF1, :]

        def stat1_out(what, part):
            return st1[:, what, part * HALF1:(part + 1) * HALF1]

        def stat1(what, part):
            return stat1_out(what, part).unsqueeze(2).broadcast_to([P, HALF1, N])

        def own_part(part):
            return own[:, part * HALF1:(part + 1) * HALF1].unsqueeze(2).broadcast_to([P, HALF1, N])

        def nbr_part(i, part):
            return blocks(nbr[i])[:, part * HALF1:(part + 1) * HALF1, :]

        def p1_blocks(g, halves):
            for heads, bk in ((slice(0, 8), bank[4 + 2 * g]), (slice(8, H1), bank[5 + 2 * g])):
                n = heads.stop - heads.start
                for b in halves:
                    r = slice(b * N, (b + 1) * N)
                    yield p1T[r, g, heads, r], bk[r, 0:n * N].rearrange("p (h q) -> p h q", q=N)

        def upto(T, k, per, n):
            return T * per + (n - k * per)

        def wait(eng, s, T, on, k, per, n):
            if on(k):
                eng.wait_ge(s, upto(T, k, per, n))

        def last(T, on, *uses):
            return [(s, upto(T, k, per, n)) for s, k, per, n in uses if on(k)][:1]

        def wait_last(eng, T, on, *uses):
            for s, v in last(T, on, *uses):
                eng.wait_ge(s, v)

        def wait_apart(eng, *waits):
            values = [(s, v if isinstance(v, int) else eng.compute_val(v)) for s, v in waits]
            eng.wait_ge(s_const, CONSTS)
            for s, v in values:
                eng.wait_ge(s, v)

        def dma_count(sems, T, par, on, k, times=1):
            c = (par + k) % 2
            return [(sems[c], T * (8 * times) + (16 * times - 8 * times * (k + c)))] if on(k) else []

        def wait_dma(eng, sems, T, par, on, k, times=1):
            for s, v in dma_count(sems, T, par, on, k, times):
                eng.wait_ge(s, v)

        def steps(eng, step):
            first = LAST + 2
            end = CHUNKS - 1
            rounds = (end - first) // 2

            def exists(t):
                return lambda k: 0 <= t - k < CHUNKS
            for t in range(first):
                step(t, t % 2, exists(t))
            with eng.Fori(0, rounds) as i:
                for half in range(2):
                    step(i * 2 + (first + half), half, lambda k: True)
            for t in range(first + 2 * rounds, CHUNKS + LAST + 1):
                step(t, t % 2, exists(t))

        block = ctx.enter_context(nc.Block())

        @block.sync
        def _(sp):
            def load_weight(n, source, after=None):
                if after is not None:
                    sp.wait_ge(s_split, after)
                sp.dma_start(stages[ORDER[n]], source.rearrange("(k p) n -> p k n", p=P)).then_inc(s_wload[n], 16)

            def load_biases():
                for col, b in ((bq_col, bq), (bk_col, bk), (bv_col, bv), (hb_col, hb)):
                    sp.dma_start(col[:, :], b.rearrange("(k p) -> p k", p=P), allow_slow_non_contiguous=True).then_inc(s_bias_load, 16)
                for q in range(HEADS_PER_TILE):
                    sp.dma_start(b1_col[q * DH1:(q + 1) * DH1, :], b1.rearrange("(e o) -> e o", o=1), allow_slow_non_contiguous=True).then_inc(s_bias_load, 16)
                sp.dma_start(bf_rep[:, :], bf.rearrange("(o n) -> o n", o=1).broadcast_to([P, D])).then_inc(s_bias_load, 16)

            def load_terms():
                sp.wait_ge(s_const, CONSTS)
                for kind, w in enumerate((w_src, w_dst)):
                    wr = w.rearrange("(f a) e -> a e f", a=HEADS_PER_TILE)
                    for q in range(HEADS_PER_TILE):
                        c = kind * HEADS_PER_TILE + (q % 2) * 2 + q // 2
                        sp.dma_start(w_terms[q * DH1:(q + 1) * DH1, :, c], wr[q], allow_slow_non_contiguous=True).then_inc(s_terms_load, 16)

            def offset(T, k):
                return (T - k) * C

            def load(T, par, on, k):
                i = (par + k) % 2
                tok = offset(T, k)
                wait(sp, s_xl, T, on, k + 2, 1, 1)
                sp.dma_start(xt[i][:, :, :], x_feat.rearrange("(k p) t -> p k t", p=P)[:, :, bass.ds(tok, C)]).then_inc(s_x_in[i], 16)
                wait(sp, s_mask, T, on, k + 2, 1, 1)
                for half in range(2):
                    sp.dma_start(adj[i][half * N:(half + 1) * N, :], adj_nodes[:, bass.ds(tok, C)]).then_inc(s_adj_in[i], 16)

            def load_tokens(T, par, on, k):
                i, tok = (par + k) % 2, offset(T, k)
                wait(sp, s_xb, T, on, k + 2, 1, 1)
                sp.dma_start(xtok[i][:, :, :], x_tok[bass.ds(tok, C), :].rearrange("(g p) n -> p g n", p=P)
                             ).then_inc(s_tok_in[i], 16)

            def load_adj1(T, par, on, k):
                i, tok = (par + k) % 2, offset(T, k)
                wait(sp, s_no_edge, T, on, k + 2, 1, 1)
                for half in range(2):
                    sp.dma_start(adj1[i][half * N:(half + 1) * N, :],
                                 adj_nodes[:, bass.ds(tok, C)]).then_inc(s_adj1_in[i], 16)

            def exchange(T, par, on, k):
                i = (par + k) % 2
                wait(sp, s_add1, T, on, k + 2, 1, 1)
                wait(sp, s_add1b, T, on, k + 2, 1, 1)
                wait(sp, s_own_t, T, on, k + 2, 1, 1)
                wait(sp, s_terms_sb, T, on, k, 1, 1)
                for f in range(KT):
                    sp.dma_start(scratch[i, f], terms[32 * f:32 * f + ROWS, :]).then_inc(s_scratch, 16)
                wait(sp, s_scratch, T, on, k, 16 * KT, 16 * KT)
                for half in range(2):
                    sp.dma_start(own_row[i][:, half * N:(half + 1) * N],
                                 scratch[i, :, 2 * half:2 * half + 2].rearrange("f u (b n) -> f (u b) n", n=N)).then_inc(s_own_row, 16)
                for half in range(2):
                    r = HEADS_PER_TILE + 2 * half
                    sp.dma_start(nbr[i][half * N:(half + 1) * N, :, :].rearrange("p (f u) t -> p f (u t)", f=KT),
                                 scratch[i, :, r:r + 2].rearrange("f u t -> f (u t)").unsqueeze(0).broadcast_to([N, KT, 2 * C])
                                 ).then_inc(s_nbr, 16)

            def step(T, par, on):
                if not isinstance(T, int):
                    for k in (-2, -1, 2, 4):
                        sp.compute_val(offset(T, k))
                        for t in range(KT):
                            sp.compute_val(offset(T, k) * 4)
                    for per, n, k in ((1, 1, 0), (1, 1, 1), (2, 2, 4), (1, 1, 4), (1, 1, 2), (16 * KT, 16 * KT, 2)):
                        sp.compute_val(upto(T, k, per, n))
                if on(-2):
                    load(T, par, on, -2)
                if on(-1):
                    load_tokens(T, par, on, -1)
                if on(2):
                    load_adj1(T, par, on, 2)
                if on(4):
                    i, tok = par, offset(T, 4)
                    wait(sp, s_res, T, on, 4, 2, 2)
                    sp.dma_start(out[bass.ds(tok, C), :].rearrange("(g p) n -> p g n", p=P),
                                 res[i][:, :, :]).then_inc(s_out[i], 16)
                if on(2):
                    exchange(T, par, on, 2)

            load_weight(0, wq)
            load(-2, 0, lambda k: k == -2, -2)
            load_weight(1, wk)
            load_biases()
            load_weight(3, wf)
            load_weight(2, wv, after=1)
            load(-1, 1, lambda k: k == -2, -2)
            load_tokens(-1, 1, lambda k: k == -1, -1)
            load_weight(4, w1, after=2)
            load_weight(5, hw_t, after=3)
            load_terms()
            steps(sp, step)
            for i in range(2):
                sp.wait_ge(s_out[i], 16 * CHUNKS // 2)

        @block.gpsimd
        def _(pool):
            pool.memset(ident[:, :], 0.0).then_inc(s_const, 1)
            pool.memset(ones[:, :], 1.0).then_inc(s_const, 1)
            pool.memset(masked_val[:, :], MASKED).then_inc(s_const, 1)
            pool.memset(w_terms[:, :, :], 0.0).then_inc(s_const, 1)
            pool.memset(power[:, :], -0.5).then_inc(s_const, 1)
            pool.memset(p0T[:, :, :, :], 0.0).then_inc(s_const, 1)
            pool.memset(p1T[:, :, :, :], 0.0).then_inc(s_const, 1)
            pool.memset(eps_first[:, :], EPS).then_inc(s_const, 1)
            pool.memset(eps_last[:, :], 4 * EPS).then_inc(s_const, 1)
            pool.memset(zero[:, :], 0.0).then_inc(s_const, 1)
            pool.wait_ge(s_const, CONSTS - 1)
            pool.affine_select(out=ident[:, :], in_=ident[:, :], compare_op=ALU.not_equal, fill=1.0, base=0,
                               pattern=[[-1, P]], channel_multiplier=1).then_inc(s_const, 1)

            def input_low(T, par, on, k):
                i = (par + k) % 2
                wait(pool, s_xh, T, on, k, 1, 1)
                wait(pool, s_v, T, on, k + 2, 2, 2)
                pool.tensor_tensor(xl[i][:, :, :], xt[i][:, :, :], xh[i][:, :, :].bitcast(F32),
                                   ALU.subtract).then_inc(s_xl, 1)

            def inverse_std(T, on, k, s_moments, s_eps, s_done, n, eps):
                wait(pool, s_moments, T, on, k, 2, 2)
                pool.tensor_tensor(ve[n][:, :], mv[n][:, :, 1], eps, ALU.add).then_inc(s_eps, 1)
                wait(pool, s_eps, T, on, k, 1, 1)
                pool.tensor_tensor(rstd[n][:, :], ve[n][:, :], power[:, :], ALU.pow).then_inc(s_done, 1)

            def step(T, par, on):
                if on(3):
                    wait(pool, s_own, T, on, 3, 1, 1)
                    wait(pool, s_nbr, T, on, 3, 32, 32)
                    wait(pool, s_t1, T, on, 4, 2, 2)
                    pool.tensor_tensor(a1_part(1), nbr_part(1 - par, 1), own_part(1), ALU.add).then_inc(s_add1b, 1)
                if on(2):
                    wait(pool, s_x1t_sb, T, on, 2, 2, 2)
                    wait(pool, s_gate, T, on, 3, 3, 3)
                    pool.tensor_tensor(x1l[:, :, :], x1T[par][:, :, :], x1h[:, :, :].bitcast(F32), ALU.subtract).then_inc(s_x1l, 1)
                if on(3):
                    for part in range(2):
                        wait(pool, s_max1, T, on, 3, 2, part + 1)
                        pool.tensor_tensor(a1_part(part), a1_part(part), stat1(0, part), ALU.subtract).then_inc(s_sub1, 1)
                if on(-1):
                    input_low(T, par, on, -1)
                if on(0):
                    wait(pool, s_max0, T, on, 0, 1, 1)
                    pool.tensor_tensor(s0_all(par), s0_all(par), stat0(par, 0), ALU.subtract).then_inc(s_sub0, 1)
                if on(3):
                    wait(pool, s_rec1, T, on, 3, 2, 2)
                    pool.tensor_tensor(a1_part(1), a1_part(1), stat1(2, 1), ALU.mult).then_inc(s_p1b, 1)
                if on(4):
                    inverse_std(T, on, 4, s_mv2, s_ve2, s_rstd2, 1, eps_last[:, :])
                    wait(pool, s_rstd2, T, on, 4, 1, 1)
                    wait(pool, s_res, T, on, 5, 2, 2)
                    pool.tensor_tensor(ve[1][:, :], mv[1][:, :, 0], rstd[1][:, :], ALU.mult).then_inc(s_mean2, 1)
                    wait(pool, s_mean2, T, on, 4, 1, 1)
                    pool.tensor_tensor(shift[:, :], zero[:, :], ve[1][:, :], ALU.subtract).then_inc(s_shift2, 1)
                if on(0):
                    wait(pool, s_rec0, T, on, 0, 1, 1)
                    pool.tensor_tensor(s0_all(par), s0_all(par), stat0(par, 2), ALU.mult).then_inc(s_p0, 1)
                if on(1):
                    inverse_std(T, on, 1, s_mv, s_ve, s_rstd, 0, eps_first[:, :])
                if on(0):
                    wait_dma(pool, s_tok_in, T, par, on, 0)
                    if not on(1):
                        pool.wait_ge(s_prep, BIAS0_READY)
                    wait(pool, s_y, T, on, 2, 2, 2)
                    pool.tensor_tensor(xb[par][:, :, :], xtok[par][:, :, :],
                                       bias0[:, :].unsqueeze(1).broadcast_to([P, G, D]), ALU.add).then_inc(s_xb, 1)

            input_low(-1, 1, lambda k: k == -1, -1)
            steps(pool, step)

        @block.scalar
        def _(act):
            act.wait_ge(s_const, CONSTS)
            def high_half(n):
                act.wait_ge(s_wload[n], 16)
                act.activation(W[ORDER[n]][0][:, :, :], stages[ORDER[n]], ACT.Copy).then_inc(s_high, 1)

            act.activation(warm[:, :], ones[:, 0:1], ACT.Exp).then_inc(s_warm, 1)
            for n in range(2):
                high_half(n)

            def input_high(T, par, on, k):
                i = (par + k) % 2
                wait_dma(act, s_x_in, T, par, on, k)
                wait(act, s_v, T, on, k + 2, 2, 2)
                act.activation(xh[i][:, :, :], xt[i][:, :, :], ACT.Copy).then_inc(s_xh, 1)

            def exp1(T, on, part):
                wait(act, s_sub1, T, on, 3, 2, part + 1)
                act.activation(a1_part(part), a1_part(part), ACT.Exp).then_inc(s_exp1, 1)

            input_high(-1, 1, lambda k: k == -1, -1)
            high_half(2)
            act.wait_ge(s_bias_load, BIAS_LOADS)
            act.wait_ge(s_prep, BIAS0_READY - 1)

            def step(T, par, on):
                if on(4):
                    for g in range(G):
                        wait(act, s_pv1, T, on, 4, 2, g + 1)
                        wait(act, s_u1, T, on, 5, 2, 2)
                        act.activation(el[:, :, g * P:(g + 1) * P], head3(bank[2 + g]), ACT.Relu,
                                       bias=b1_neg[:, :], scale=-1.0).then_inc(s_neg, 1)
                    wait(act, s_neg, T, on, 4, 2, 2)
                    act.activation(el[:, :, :], el[:, :, :], ACT.Exp, scale=-1.0).then_inc(s_el, 1)
                if on(0):
                    for m in range(KT):
                        wait(act, s_qk, T, on, 0, 3, m + 1)
                        wait(act, s_s0, T, on, 1, 2, 2)
                        b = bank[m % 2]
                        act.activation(qT[:, m, :], b[:, 0:C], ACT.Identity, bias=bq_col[:, m:m + 1]).then_inc(s_qk_sb, 1)
                        act.activation(kT[:, m, :], b[:, C:2 * C], ACT.Identity, bias=bk_col[:, m:m + 1]).then_inc(s_qk_sb, 1)
                    if not on(1):
                        for n in range(3, len(ORDER)):
                            high_half(n)
                if on(2):
                    for g in range(G):
                        wait(act, s_x1t, T, on, 2, 2, g + 1)
                        wait(act, s_gate, T, on, 3, 3, 3)
                        act.activation(x1h[:, :, g * P:(g + 1) * P], head3(bank[2 + g]), ACT.Copy).then_inc(s_x1h, 1)
                    for g in range(G):
                        wait(act, s_z, T, on, 4, 1, 1)
                        act.activation(x1T[par][:, :, g * P:(g + 1) * P], head3(bank[2 + g]), ACT.Copy).then_inc(s_x1t_sb, 1)
                if on(0):
                    for g in range(G):
                        wait(act, s_v, T, on, 0, 2, g + 1)
                        wait(act, s_pv0, T, on, 2, 2, g + 1)
                        act.activation(v[par][:, g, :], bank[1 - g][:, 0:D], ACT.Copy).then_inc(s_v_sb, 1)
                if on(1):
                    for g in range(G):
                        wait(act, s_t0, T, on, 1, 2, g + 1)
                        wait(act, s_pv0, T, on, 2, 2, g + 1)
                        for b in range(2):
                            r = slice(b * N, (b + 1) * N)
                            act.activation(p0T[r, g, :, r], bank[2 + g][r, 0:J0 * P].rearrange("p (h q) -> p h q", q=N),
                                           ACT.Copy).then_inc(s_t0_sb, 1)
                if on(3):
                    exp1(T, on, 0)
                if on(-1):
                    input_high(T, par, on, -1)
                if on(1):
                    for g in range(G):
                        wait(act, s_pv0, T, on, 1, 2, g + 1)
                        wait(act, s_wf, T, on, 2, 2, g + 1)
                        act.activation(ch[:, g, :, :], head3(bank[6 + g]), ACT.Copy).then_inc(s_ch, 1)
                if on(3):
                    exp1(T, on, 1)
                if on(2):
                    for g in range(G):
                        wait(act, s_h, T, on, 2, 2, g + 1)
                        wait(act, s_pv1, T, on, 4, 2, g + 1)
                        act.activation(h[par][:, g, :], bank[1 - g][:, 0:D], ACT.Copy).then_inc(s_h_sb, 1)
                if on(0):
                    wait(act, s_sub0, T, on, 0, 1, 1)
                    act.activation(s0_all(par), s0_all(par), ACT.Exp).then_inc(s_exp0, 1)
                if on(2):
                    for g in range(G):
                        wait(act, s_ht, T, on, 2, 2, g + 1)
                        wait(act, s_terms, T, on, 3, 1, 1)
                        act.activation(thT[:, :, g * P:(g + 1) * P], head3(bank[2 + g]), ACT.Tanh).then_inc(s_th, 1)
                if on(4):
                    wait(act, s_shift2, T, on, 4, 1, 1)
                    wait_dma(act, s_out, T, par, on, 6)
                    for g in range(G):
                        act.activation(res[par][:, g, :], bank[6 + g][:, 0:D], ACT.Identity,
                                       bias=shift[:, g:g + 1], scale=rstd[1][:, g:g + 1]).then_inc(s_res, 1)
                for m in range(KT):
                    if on(2):
                        wait(act, s_gate, T, on, 2, 3, m + 1)
                        wait(act, s_gated, T, on, 4, 1, 1)
                        act.activation(gate[par][:, m, :], bank[1 - m % 2][:, 0:C], ACT.Tanh,
                                       bias=hb_half[:, m:m + 1], scale=0.5).then_inc(s_gate_sb, 1)
                    if on(2) and m == 0:
                        wait(act, s_terms, T, on, 2, 1, 1)
                        wait(act, s_scratch, T, on, 3, 16 * KT, 16 * KT)
                        act.activation(terms[0:96, :], bank[3][0:96, 0:C], ACT.Copy).then_inc(s_terms_sb, 1)
                    if on(3) and m < G:
                        wait(act, s_t1, T, on, 3, 2, m + 1)
                        wait(act, s_pv1, T, on, 4, 2, m + 1)
                        for out_ap, in_ap in p1_blocks(m, (0, 1) if m == 0 else (0,)):
                            act.activation(out_ap, in_ap, ACT.Copy).then_inc((s_t1_sb, s_t1b_sb)[m], 1)

            steps(act, step)

        @block.vector
        def _(dve):
            def low_half(n):
                hi, lo = W[ORDER[n]]
                dve.wait_ge(s_high, n + 1)
                dve.tensor_tensor(lo[:, :, :], stages[ORDER[n]], hi[:, :, :].bitcast(F32), ALU.subtract).then_inc(s_split, 1)

            def mask0(T, par, on, k):
                i = (par + k) % 2
                wait_dma(dve, s_adj_in, T, par, on, k, 2)
                wait(dve, s_s0_sb, T, on, k + 2, 2, 2)
                dve.tensor_scalar(bias_m[i][:, :], adj[i][:, :], 1.0, NEG, ALU.subtract, ALU.mult).then_inc(s_mask, 1)

            def residual(T, par, on, g):
                wait(dve, s_wf, T, on, 1, 2, g + 1)
                wait(dve, s_xb, T, on, 1, 1, 1)
                wait(dve, s_x1, T, on, 2, 2, 2)
                dve.tensor_tensor(y[:, g, :], bank[1 - g][:, 0:D], xb[1 - par][:, g, :], ALU.add).then_inc(s_y, 1)

            def step(T, par, on):
                if on(4):
                    for g in range(G):
                        wait(dve, s_el, T, on, 4, 1, 1)
                        wait(dve, s_gated, T, on, 5, 1, 1)
                        wait(dve, s_z, T, on, 5, 1, 1)
                        dve.scalar_tensor_tensor(u[:, :, g * P:(g + 1) * P], el[:, :, g * P:(g + 1) * P], b1_neg1[:, :],
                                                 head3(bank[2 + g]), ALU.add, ALU.max).then_inc(s_u1, 1)
                    wait(dve, s_u1, T, on, 4, 2, 2)
                    dve.scalar_tensor_tensor(u[:, :, :], u[:, :, :], b1_col[:, :], x1T[par][:, :, :],
                                             ALU.add, ALU.subtract).then_inc(s_u2, 1)
                if on(3):
                    wait_dma(dve, s_adj1_in, T, par, on, 3, 2)
                    wait(dve, s_msk1, T, on, 4, 2, 2)
                    dve.tensor_scalar(no_edge[:, :], adj1[1 - par][:, :], 0.0, None, ALU.is_equal).then_inc(s_no_edge, 1)
                    wait(dve, s_own_t, T, on, 3, 1, 1)
                    wait(dve, s_add1b, T, on, 4, 1, 1)
                    dve.tensor_copy(own[:, :], bank[6][:, 0:J1 * B]).then_inc(s_own, 1)
                if on(4):
                    wait(dve, s_u2, T, on, 4, 1, 1)
                    wait(dve, s_gate_sb, T, on, 4, 3, 3)
                    dve.scalar_tensor_tensor(u[:, :, :], gate[par][:, :, :], 1.0, u[:, :, :],
                                             ALU.add, ALU.mult).then_inc(s_gated, 1)
                if on(3):
                    wait(dve, s_own, T, on, 3, 1, 1)
                    wait(dve, s_nbr, T, on, 3, 32, 32)
                    wait(dve, s_t1, T, on, 4, 2, 2)
                    dve.tensor_tensor(a1_part(0), nbr_part(1 - par, 0), own_part(0), ALU.add).then_inc(s_add1, 1)
                if on(4):
                    wait(dve, s_gated, T, on, 4, 1, 1)
                    wait(dve, s_zt, T, on, 5, 2, 2)
                    dve.scalar_tensor_tensor(z[:, :, :], x1T[par][:, :, :], 4.0, u[:, :, :],
                                             ALU.mult, ALU.add).then_inc(s_z, 1)
                if on(3):
                    for part in range(2):
                        wait(dve, (s_add1, s_add1b)[part], T, on, 3, 1, 1)
                        dve.scalar_tensor_tensor(a1_part(part), a1_part(part), ALPHA, a1_part(part),
                                                 ALU.mult, ALU.max).then_inc(s_lrelu, 1)
                        j = slice(part * J1 // 2, (part + 1) * J1 // 2)
                        wait_apart(dve, *last(T, on, (s_lrelu, 3, 2, part + 1)), *last(T, on, (s_no_edge, 3, 1, 1)))
                        dve.copy_predicated(a1[:, j, :], no_edge[:, :].unsqueeze(1).broadcast_to([P, J1 // 2, C]),
                                            masked_val[:, :].unsqueeze(2).broadcast_to([P, J1 // 2, C])).then_inc(s_msk1, 1)
                        wait(dve, s_msk1, T, on, 3, 2, part + 1)
                        dve.tensor_reduce(stat1_out(0, part), a1_part(part), AX.X, ALU.max).then_inc(s_max1, 1)
                if on(0):
                    for g in range(G):
                        wait(dve, s_s0, T, on, 0, 2, g + 1)
                        wait(dve, s_mask, T, on, 0, 1, 1)
                        wait(dve, s_t0, T, on, 2, 2, 2)
                        dve.scalar_tensor_tensor(s0[par][:, g, :].rearrange("p (j c) -> p j c", c=P), head3(bank[4 + g]), SCALE,
                                                 bias_m[par][:, g * P:(g + 1) * P].unsqueeze(1).broadcast_to([P, J0, P]),
                                                 ALU.mult, ALU.add).then_inc(s_s0_sb, 1)
                if on(3):
                    wait(dve, s_exp1, T, on, 3, 2, 1)
                    dve.tensor_reduce(stat1_out(1, 0), a1_part(0), AX.X, ALU.add).then_inc(s_sum1, 1)
                if on(1):
                    for g in range(G):
                        wait(dve, s_ch, T, on, 1, 2, g + 1)
                        wait(dve, s_wf, T, on, 2, 2, g + 1)
                        dve.tensor_tensor(cl[:, g, :, :], head3(bank[6 + g]), ch[:, g, :, :].bitcast(F32), ALU.subtract).then_inc(s_cl, 1)
                if on(0):
                    wait(dve, s_s0_sb, T, on, 0, 2, 2)
                    dve.tensor_reduce(stat0_out(par, 0), s0_all(par), AX.X, ALU.max).then_inc(s_max0, 1)
                if on(3):
                    wait(dve, s_exp1, T, on, 3, 2, 2)
                    dve.tensor_reduce(stat1_out(1, 1), a1_part(1), AX.X, ALU.add).then_inc(s_sum1, 1)
                    for part in range(2):
                        wait(dve, s_sum1, T, on, 3, 2, part + 1)
                        dve.reciprocal(stat1_out(2, part), stat1_out(1, part)).then_inc(s_rec1, 1)
                if on(4):
                    for g in range(G):
                        wait(dve, s_zt, T, on, 4, 2, g + 1)
                        dve.bn_stats(ln[1][:, g, :], bank[6 + g][:, 0:D]).then_inc(s_bn2, 1)
                    for g in range(G):
                        wait_apart(dve, *last(T, on, (s_bn2, 4, 2, g + 1)), *last(T, on, (s_res, 5, 2, 2)))
                        dve.bn_aggr(mv[1][:, g, :], ln[1][:, g, :]).then_inc(s_mv2, 1)
                if on(1):
                    residual(T, par, on, 0)
                if on(3):
                    wait(dve, s_rec1, T, on, 3, 2, 1)
                    dve.tensor_tensor(a1_part(0), a1_part(0), stat1(2, 0), ALU.mult).then_inc(s_p1a, 1)
                if on(1):
                    residual(T, par, on, 1)
                if on(0):
                    wait(dve, s_exp0, T, on, 0, 1, 1)
                    dve.tensor_reduce(stat0_out(par, 1), s0_all(par), AX.X, ALU.add).then_inc(s_sum0, 1)
                    wait(dve, s_sum0, T, on, 0, 1, 1)
                    dve.reciprocal(stat0_out(par, 2), stat0_out(par, 1)).then_inc(s_rec0, 1)
                if on(1):
                    for g in range(G):
                        wait(dve, s_y, T, on, 1, 2, g + 1)
                        dve.bn_stats(ln[0][:, g, :], y[:, g, :]).then_inc(s_bn, 1)
                    for g in range(G):
                        wait_apart(dve, *last(T, on, (s_bn, 1, 2, g + 1)))
                        dve.bn_aggr(mv[0][:, g, :], ln[0][:, g, :]).then_inc(s_mv, 1)
                if on(-1):
                    mask0(T, par, on, -1)
                if on(3):
                    wait(dve, s_t1, T, on, 3, 2, 2)
                    wait(dve, s_pv1, T, on, 4, 2, 2)
                    for out_ap, in_ap in p1_blocks(1, (1,)):
                        dve.tensor_copy(out_ap, in_ap).then_inc(s_t1b_sb, 1)
                if on(1):
                    wait(dve, s_rstd, T, on, 1, 1, 1)
                    wait(dve, s_x1t, T, on, 2, 2, 2)
                    for g in range(G):
                        dve.tensor_scalar(x1[:, g, :], y[:, g, :], mv[0][:, g, 0:1], rstd[0][:, g:g + 1],
                                          ALU.subtract, ALU.mult).then_inc(s_x1, 1)

            for n in range(2):
                low_half(n)
            dve.wait_ge(s_bias_load, BIAS_LOADS)
            dve.wait_ge(s_const, CONSTS)
            for k in range(KT):
                dve.tensor_scalar(bv_rep[:, k, :], ones[:, :], bv_col[:, k:k + 1], None, ALU.mult).then_inc(s_prep, 1)
            dve.tensor_scalar(hb_half[:, :], hb_col[:, :], 0.5, None, ALU.mult).then_inc(s_prep, 1)
            dve.tensor_scalar(b1_neg[:, :], b1_col[:, :], -1.0, None, ALU.mult).then_inc(s_prep, 1)
            dve.tensor_scalar(b1_neg1[:, :], b1_col[:, :], -1.0, -1.0, ALU.mult, ALU.add).then_inc(s_prep, 1)
            mask0(-1, 1, lambda k: k == -1, -1)
            for n in range(2, len(ORDER)):
                low_half(n)
            dve.wait_ge(s_prep_mm, 1)
            dve.tensor_tensor(bias0[:, :], bank[7][:, 0:D], bf_rep[:, :], ALU.add).then_inc(s_prep, 1)
            steps(dve, step)

        @block.tensor
        def _(pe):
            def product(out_ap, left, right):
                for k in range(KT):
                    (lh, ll), (rh, rl) = left(k), right(k)
                    pe.matmul(out_ap, lh, rh, start=(k == 0), stop=False)
                    pe.matmul(out_ap, lh, rl, start=False, stop=False)
                    mm = pe.matmul(out_ap, ll, rh, start=False, stop=(k == KT - 1))
                return mm

            def weight(name, cols):
                return lambda k: tuple(w[:, k, cols] for w in W[name])

            def tokens(hi, lo, cols):
                return lambda k: (hi[:, k, cols], lo[:, k, cols])

            def bias_product():
                pe.wait_ge(s_prep, KT)
                pe.wait_ge(s_wload[ORDER.index("wf")], 16)
                for k in range(KT):
                    mm = pe.matmul(bank[7][:, 0:D], bv_rep[:, k, :], wf_full[:, k, :], start=(k == 0), stop=(k == KT - 1))
                mm.then_inc(s_prep_mm, 1)

            def step(T, par, on):
                prev = 1 - par
                for m in range(KT):
                    if on(0):
                        if not on(1):
                            pe.wait_ge(s_split, 2)
                        wait(pe, s_xl, T, on, 0, 1, 1)
                        if m == 0:
                            wait_last(pe, T, on, (s_gate_sb, 3, 3, 2), (s_y, 2, 2, 2), (s_v_sb, 1, 2, 2))
                        elif m == 1:
                            wait_last(pe, T, on, (s_gate_sb, 3, 3, 3), (s_y, 2, 2, 1), (s_v_sb, 1, 2, 1))
                        else:
                            wait(pe, s_qk_sb, T, on, 0, 6, 2)
                        fm = slice(m * P, (m + 1) * P)
                        b = bank[m % 2]
                        product(b[:, 0:C], weight("wq", fm), tokens(xh[par], xl[par], slice(0, C)))
                        product(b[:, C:2 * C], weight("wk", fm), tokens(xh[par], xl[par], slice(0, C))).then_inc(s_qk, 1)
                    if on(3) and m == 1:
                        wait(pe, s_own_row, T, on, 3, 32, 32)
                        wait(pe, s_t1b_sb, T, on, 4, 4, 4)
                        pe.matmul(bank[6][:, 0:J1 * B], own_row[prev][:, :], ident[0:J1 * B, 0:J1 * B],
                                  start=True, stop=True).then_inc(s_own_t, 1)
                if on(2):
                    for g in range(G):
                        wait(pe, s_x1, T, on, 2, 2, g + 1)
                        wait_last(pe, T, on, (s_u1, 4, 2, 2), (s_terms_sb, 3, 1, 1), (s_t0_sb, 2, 4, 2 * g + 2))
                        for f in range(KT):
                            mm = pe.transpose(bank[2 + g][:, f * P:(f + 1) * P], x1[:, g, f * P:(f + 1) * P], ident[:, :])
                        mm.then_inc(s_x1t, 1)
                if on(0):
                    if not on(1):
                        pe.wait_ge(s_split, 3)
                    wait_last(pe, T, on, (s_t1_sb, 4, 4, 4), (s_s0_sb, 1, 2, 2))
                    for g in range(G):
                        wait(pe, s_qk_sb, T, on, 0, 6, 4 + 2 * g)
                        product(bank[1 - g][:, 0:D], tokens(xh[par], xl[par], slice(g * P, (g + 1) * P)),
                                weight("wv", slice(0, D))).then_inc(s_v, 1)
                if on(1):
                    wait(pe, s_p0, T, on, 1, 1, 1)
                    for g in range(G):
                        wait(pe, s_x1t_sb, T, on, 2, 2, g + 1)
                        for j in range(J0):
                            mm = pe.transpose(bank[2 + g][:, j * P:(j + 1) * P], s0[prev][:, g, j * P:(j + 1) * P], ident[:, :])
                        mm.then_inc(s_t0, 1)
                if on(0):
                    for g in range(G):
                        for j in range(J0):
                            for b in range(2):
                                t = slice(g * P + b * N, g * P + (b + 1) * N)
                                for half in range(2):
                                    r = slice(half * DH0, (half + 1) * DH0)
                                    mm = pe.matmul(bank[4 + g][r, (2 * j + b) * N:(2 * j + b + 1) * N],
                                                   qT[r, j, t], kT[r, j, t], start=True, stop=True)
                        mm.then_inc(s_s0, 1)
                    if not on(1):
                        bias_product()
                if on(1):
                    wait(pe, s_v_sb, T, on, 1, 2, 2)
                    for g in range(G):
                        wait(pe, s_t0_sb, T, on, 1, 4, 2 * g + 2)
                        if g == 0:
                            wait_last(pe, T, on, (s_own, 3, 1, 1), (s_cl, 2, 2, 1))
                        else:
                            wait_last(pe, T, on, (s_t1b_sb, 4, 4, 4), (s_cl, 2, 2, 2))
                        for head in range(H0):
                            r, c = head % 2 * DH0, head * DH0
                            mm = pe.matmul(bank[6 + g][r:r + DH0, head // 2 * P:(head // 2 + 1) * P],
                                           v[prev][:, g, c:c + DH0], p0T[:, g, head, :], start=True, stop=True)
                        mm.then_inc(s_pv0, 1)
                if on(2):
                    if not on(3):
                        pe.wait_ge(s_split, len(ORDER))
                        pe.wait_ge(s_terms_load, 16 * 2 * HEADS_PER_TILE)
                    wait(pe, s_x1l, T, on, 2, 1, 1)
                    for g in range(G):
                        wait_last(pe, T, on, (s_v_sb, 0, 2, g + 1), (s_gate_sb, 3, 3, 3 - g))
                        product(bank[1 - g][:, 0:D], tokens(x1h, x1l, slice(g * P, (g + 1) * P)),
                                weight("w1", slice(0, D))).then_inc(s_h, 1)
                if on(4):
                    wait(pe, s_z, T, on, 4, 1, 1)
                    for g in range(G):
                        wait_last(pe, T, on, (s_cl, 1, 2, g + 1), (s_own, 3, 1, 1), (s_t1b_sb, 4, 4, 4))
                        for f in range(KT):
                            mm = pe.transpose(bank[6 + g][:, f * P:(f + 1) * P], z[:, f, g * P:(g + 1) * P], ident[:, :])
                        mm.then_inc(s_zt, 1)
                if on(1):
                    if not on(2):
                        pe.wait_ge(s_split, 4)
                    for g in range(G):
                        wait(pe, s_cl, T, on, 1, 2, g + 1)
                        wait_last(pe, T, on, (s_h_sb, 2, 2, g + 1), (s_v_sb, 0, 2, g + 1))
                        product(bank[1 - g][:, 0:D], lambda j: (ch[:, g, j, :], cl[:, g, j, :]),
                                weight("wf", slice(0, D))).then_inc(s_wf, 1)
                if on(2):
                    for g in range(G):
                        wait(pe, s_h_sb, T, on, 2, 2, g + 1)
                        wait_last(pe, T, on, (s_t0_sb, 1, 4, 2 * g + 2), (s_x1t_sb, 2, 2, g + 1))
                        for f in range(KT):
                            mm = pe.transpose(bank[2 + g][:, f * P:(f + 1) * P], h[par][:, g, f * P:(f + 1) * P], ident[:, :])
                        mm.then_inc(s_ht, 1)
                for m in range(KT):
                    if on(2):
                        if m < 2:
                            wait_last(pe, T, on, (s_y, 1, 2, m + 1), (s_h_sb, 2, 2, m + 1))
                        else:
                            wait(pe, s_gate_sb, T, on, 2, 3, 1)
                        product(bank[1 - m % 2][:, 0:C], weight("hw", slice(m * P, (m + 1) * P)),
                                tokens(x1h, x1l, slice(0, C))).then_inc(s_gate, 1)
                    if on(2) and m == 0:
                        wait(pe, s_th, T, on, 2, 2, 2)
                        for f in range(KT):
                            mm = pe.matmul(bank[3][32 * f:32 * f + 32, 0:C], w_terms[:, f, :], thT[:, f, :], start=True, stop=True)
                        mm.then_inc(s_terms, 1)
                    if on(3) and m < G:
                        g = m
                        wait(pe, s_p1a, T, on, 3, 1, 1)
                        wait(pe, s_p1b, T, on, 3, 1, 1)
                        if g == 0:
                            wait_last(pe, T, on, (s_s0_sb, 0, 2, 2), (s_t1_sb, 4, 4, 4))
                        else:
                            wait_last(pe, T, on, (s_res, 4, 2, 2), (s_cl, 1, 2, 2), (s_own, 3, 1, 1))
                        for j in range(J1):
                            mm = pe.transpose(bank[4 + 2 * g + j // 4][:, j % 4 * P:(j % 4 + 1) * P],
                                              a1[:, j, g * P:(g + 1) * P], ident[:, :])
                        mm.then_inc(s_t1, 1)
                if on(3):
                    for g in range(G):
                        wait(pe, (s_t1_sb, s_t1b_sb)[g], T, on, 3, 4, 4)
                        wait_last(pe, T, on, (s_th, 2, 2, 1) if g == 0 else (s_terms_sb, 2, 1, 1), (s_u1, 4, 2, 2))
                        for head in range(H1):
                            r = head % HEADS_PER_TILE * DH1
                            mm = pe.matmul(bank[2 + g][r:r + DH1, head // HEADS_PER_TILE * P:(head // HEADS_PER_TILE + 1) * P],
                                           h[prev][:, g, head * DH1:(head + 1) * DH1], p1T[:, g, head, :], start=True, stop=True)
                        mm.then_inc(s_pv1, 1)

            pe.wait_ge(s_const, CONSTS)
            steps(pe, step)


INS = ("x_tok", "x_feat", "adj_nodes", "wq", "bq", "wk", "bk", "wv", "bv", "wf", "bf",
       "w1", "b1", "w_src", "w_dst", "hw_t", "hb")


def kernel(x, adj, L0_gnn_Wq, L0_gnn_bq, L0_gnn_Wk, L0_gnn_bk, L0_gnn_Wv, L0_gnn_bv, L0_gnn_Wf, L0_gnn_bf,
           L1_gnn_W, L1_gnn_b, L1_gnn_w_src, L1_gnn_w_dst, L1_gnn_H_w, L1_gnn_H_b):
    import concourse.bacc as bacc
    from concourse.bass_utils import run_bass_kernel_spmd

    graphs, nodes, dim = x.shape
    x_tok = np.ascontiguousarray(np.asarray(x).reshape(graphs * nodes, dim))
    edges = np.ascontiguousarray(np.asarray(adj).transpose(1, 0, 2)).reshape(nodes, graphs * nodes)
    arrays = dict(zip(INS, (
        x_tok, np.ascontiguousarray(x_tok.T), edges,
        L0_gnn_Wq, L0_gnn_bq, L0_gnn_Wk, L0_gnn_bk, L0_gnn_Wv, L0_gnn_bv, L0_gnn_Wf, L0_gnn_bf,
        np.ascontiguousarray(np.asarray(L1_gnn_W).transpose(1, 0, 2)).reshape(dim, dim),
        L1_gnn_b, np.asarray(L1_gnn_w_src)[:, :, 0], np.asarray(L1_gnn_w_dst)[:, :, 0],
        np.ascontiguousarray(np.asarray(L1_gnn_H_w).T), L1_gnn_H_b)))
    arrays = {n: np.ascontiguousarray(a) for n, a in arrays.items()}
    nc = bacc.Bacc("TRN2", target_bir_lowering=False, num_devices=1)
    args = [nc.dram_tensor(n, a.shape, mybir.dt.from_np(a.dtype), kind="ExternalInput").ap() for n, a in arrays.items()]
    out = nc.dram_tensor("out", x_tok.shape, mybir.dt.float32, kind="ExternalOutput").ap()
    graph_attention_pair(nc, *args, out)
    result = run_bass_kernel_spmd(nc, [arrays], core_ids=[0])
    return result.results[0]["out"].reshape(graphs, nodes, dim)
```
